# Optimizing a Trainium2 kernel written in Bass

```python
import numpy as np
import jax
import jax.numpy as jnp

def _softmax(x, axis=-1):
    return jax.nn.softmax(x, axis=axis)

def _gelu(x):
    return jax.nn.gelu(x, approximate=True)

def _silu(x):
    return jax.nn.silu(x)

def _sigmoid(x):
    return jax.nn.sigmoid(x)

def _layernorm(x, axis=-1, eps=1e-05):
    m = jnp.mean(x, axis=axis, keepdims=True)
    v = jnp.var(x, axis=axis, keepdims=True)
    return (x - m) / jnp.sqrt(v + eps)

def _scatter_add(tgt, idx, src, axis=0):
    return tgt.at[idx].add(src)

def _segment_sum(src, seg, n):
    return jax.ops.segment_sum(src, seg, n)
kernel_name = 'mk_conv_attn_hybrid_d2_conv_nchw512_r4_80571e'

def setup_inputs(seed: int=0):
    np.random.seed(seed)
    _w = jnp.asarray

    def _rec_inputs():
        import jax
        import jax.numpy as jnp
        _gk = jax.random.key(seed)
        x = -0.0002928 + 1 * jax.random.normal(jax.random.fold_in(_gk, 1), (8, 128, 32, 32), jnp.float32)
        return x
    x = _rec_inputs()

    def _L0_conv_setup():
        import jax, jax.numpy as jnp
        import numpy as np
        NUM_HEADS = 8
        HEAD_DIM = 16
        SCALE = HEAD_DIM ** (-0.5)
        key = jax.random.key(seed)
        k_x, k_wp, k_bp, k_wo, k_bo = jax.random.split(key, 5)
        C = 128
        inner = NUM_HEADS * HEAD_DIM
        return {'x': jax.random.normal(k_x, (8, C, 32, 32), dtype=jnp.float32), 'w_proj': jax.random.normal(k_wp, (C, 3 * inner), dtype=jnp.float32) * C ** (-0.5), 'b_proj': jax.random.normal(k_bp, (3 * inner,), dtype=jnp.float32) * 0.02, 'w_out': jax.random.normal(k_wo, (inner, C), dtype=jnp.float32) * inner ** (-0.5), 'b_out': jax.random.normal(k_bo, (C,), dtype=jnp.float32) * 0.02}
    _L0_conv_all = _L0_conv_setup()
    _L0_conv_in = {k: v for k, v in _L0_conv_all.items() if k in ('w_proj', 'b_proj', 'w_out', 'b_out')}
    del _L0_conv_all

    def _L1_attn_setup():
        import jax, jax.numpy as jnp
        import numpy as np
        Q_THRESH = 0.25
        K_THRESH = 0.25
        V_THRESH = 0.3
        MASK_THRESH = 0.1
        NEG_INF = -1000000000.0

        def _spike(u, threshold):
            return (u >= threshold).astype(u.dtype)
        key = jax.random.key(seed)
        k1, k2, k3, k4 = jax.random.split(key, 4)
        B, L, D = (4, 1024, 128)
        x_seq = jax.random.normal(k1, (B, L, D), dtype=jnp.float32)
        Wq = jax.random.normal(k2, (D, D), dtype=jnp.float32) / np.sqrt(D)
        Wk = jax.random.normal(k3, (D, D), dtype=jnp.float32) / np.sqrt(D)
        Wv = jax.random.normal(k4, (D, D), dtype=jnp.float32) / np.sqrt(D)
        return {'x_seq': x_seq, 'Wq': Wq, 'Wk': Wk, 'Wv': Wv}
    _L1_attn_all = _L1_attn_setup()
    _L1_attn_in = {k: v for k, v in _L1_attn_all.items() if k in ('Wq', 'Wk', 'Wv')}
    del _L1_attn_all

    def _L1_ffn_setup():
        import jax, jax.numpy as jnp
        import numpy as np
        E, D, H = (8, 128, 512)
        B, N = (8, 128)
        key = jax.random.key(seed)
        ks = jax.random.split(key, 4)

        def init(k, shape, fan_in):
            return jax.random.normal(k, shape, jnp.float32) * (1.0 / np.sqrt(fan_in))
        return {'x': jax.random.normal(ks[0], (B, N, D), jnp.float32), 'Wr': init(ks[1], (D, E), D), 'br': jnp.zeros((E,), jnp.float32), 'W1': init(ks[2], (E, D, H), D), 'b1': jnp.zeros((E, H), jnp.float32), 'W2': init(ks[3], (E, H, D), H), 'b2': jnp.zeros((E, D), jnp.float32)}
    _L1_ffn_all = _L1_ffn_setup()
    _L1_ffn_in = {k: v for k, v in _L1_ffn_all.items() if k in ('Wr', 'br', 'W1', 'b1', 'W2', 'b2')}
    del _L1_ffn_all
    return {'x': x, 'L0_conv_w_proj': _L0_conv_in['w_proj'], 'L0_conv_b_proj': _L0_conv_in['b_proj'], 'L0_conv_w_out': _L0_conv_in['w_out'], 'L0_conv_b_out': _L0_conv_in['b_out'], 'L1_attn_Wq': _L1_attn_in['Wq'], 'L1_attn_Wk': _L1_attn_in['Wk'], 'L1_attn_Wv': _L1_attn_in['Wv'], 'L1_ffn_Wr': _L1_ffn_in['Wr'], 'L1_ffn_br': _L1_ffn_in['br'], 'L1_ffn_W1': _L1_ffn_in['W1'], 'L1_ffn_b1': _L1_ffn_in['b1'], 'L1_ffn_W2': _L1_ffn_in['W2'], 'L1_ffn_b2': _L1_ffn_in['b2']}

def reference(x, L0_conv_w_proj, L0_conv_b_proj, L0_conv_w_out, L0_conv_b_out, L1_attn_Wq, L1_attn_Wk, L1_attn_Wv, L1_ffn_Wr, L1_ffn_br, L1_ffn_W1, L1_ffn_b1, L1_ffn_W2, L1_ffn_b2):
    import jax
    import jax.numpy as jnp

    def _L0_conv_ref(x, w_proj, b_proj, w_out, b_out):
        import jax, jax.numpy as jnp
        import numpy as np
        NUM_HEADS = 8
        HEAD_DIM = 16
        SCALE = HEAD_DIM ** (-0.5)
        B, C, H, W = x.shape
        N = H * W
        tokens = x.reshape(B, C, N).transpose(0, 2, 1)
        qkv = (tokens @ w_proj + b_proj).reshape(B, N, NUM_HEADS, 3 * HEAD_DIM)
        q, k, v = jnp.split(qkv, 3, axis=-1)
        attn = jnp.einsum('bihd,bjhd->bijh', q, k) * SCALE
        attn = jax.nn.softmax(attn, axis=2)
        res = jnp.einsum('bijh,bjhd->bihd', attn, v).reshape(B, N, NUM_HEADS * HEAD_DIM)
        out = res @ w_out + b_out + tokens
        return out.transpose(0, 2, 1).reshape(B, C, H, W)

    def _L1_attn_ref(x_seq, Wq, Wk, Wv):
        import jax, jax.numpy as jnp
        import numpy as np
        Q_THRESH = 0.25
        K_THRESH = 0.25
        V_THRESH = 0.3
        MASK_THRESH = 0.1
        NEG_INF = -1000000000.0

        def _spike(u, threshold):
            return (u >= threshold).astype(u.dtype)
        B, L, D = x_seq.shape
        u_q = jnp.einsum('bld,ed->ble', x_seq, Wq)
        u_k = jnp.einsum('bld,ed->ble', x_seq, Wk)
        u_v = jnp.einsum('bld,ed->ble', x_seq, Wv)
        s_q = _spike(u_q, Q_THRESH)
        s_k = _spike(u_k, K_THRESH)
        s_v = _spike(u_v, V_THRESH)
        score = jnp.einsum('bld,bmd->blm', s_q, s_k)
        causal = jnp.triu(jnp.ones((L, L), dtype=bool), k=1)
        score = jnp.where(causal, NEG_INF, score)
        router_mask = (score > MASK_THRESH).astype(x_seq.dtype)
        out_spike = jnp.einsum('blm,bmd->bld', router_mask, s_v)
        return out_spike

    def _L1_ffn_ref(x, Wr, br, W1, b1, W2, b2):
        import jax, jax.numpy as jnp
        import numpy as np
        E, D, H = (8, 128, 512)
        B, N = (8, 128)
        b, n, d = x.shape
        xt = x.reshape(-1, d)
        route_prob = jax.nn.softmax(xt.astype(jnp.float32) @ Wr + br, axis=-1)
        routes = jnp.argmax(route_prob, axis=-1)
        p_max = jnp.max(route_prob, axis=-1)

        def expert_step(acc, inp):
            w1, bb1, w2, bb2, e = inp
            h = jax.nn.gelu(xt @ w1 + bb1, approximate=False)
            y = h @ w2 + bb2
            return (acc + y * (routes == e)[:, None].astype(y.dtype), None)
        out, _ = jax.lax.scan(expert_step, jnp.zeros_like(xt), (W1, b1, W2, b2, jnp.arange(E)))
        out = out * (p_max / jax.lax.stop_gradient(p_max))[:, None]
        return out.reshape(b, n, d)

    def _gn(v, G=32, eps=1e-05):
        B_, C_, H_, W_ = v.shape
        g = v.reshape(B_, G, C_ // G, H_, W_)
        m = jnp.mean(g, axis=(2, 3, 4), keepdims=True)
        s = jnp.var(g, axis=(2, 3, 4), keepdims=True)
        return ((g - m) / jnp.sqrt(s + eps)).reshape(v.shape)

    def _ln_c(v, eps=1e-06):
        m = jnp.mean(v, axis=1, keepdims=True)
        s = jnp.var(v, axis=1, keepdims=True)
        return (v - m) / jnp.sqrt(s + eps)

    def _ln_t(v, eps=1e-05):
        m = jnp.mean(v, axis=-1, keepdims=True)
        s = jnp.var(v, axis=-1, keepdims=True)
        return (v - m) / jnp.sqrt(s + eps)

    def _to_tokens(v):
        B_, C_, H_, W_ = v.shape
        return v.reshape(B_, C_, H_ * W_).transpose(0, 2, 1)

    def _from_tokens(t, like):
        B_, C_, H_, W_ = like.shape
        return t.transpose(0, 2, 1).reshape(B_, C_, H_, W_)
    x = _L0_conv_ref(x, L0_conv_w_proj, L0_conv_b_proj, L0_conv_w_out, L0_conv_b_out)
    t = _to_tokens(x)
    t = t + _L1_attn_ref(_ln_t(t), L1_attn_Wq, L1_attn_Wk, L1_attn_Wv)
    t = t + _L1_ffn_ref(_ln_t(t), L1_ffn_Wr, L1_ffn_br, L1_ffn_W1, L1_ffn_b1, L1_ffn_W2, L1_ffn_b2)
    x = _from_tokens(t, x)
    return x

_drawn_inputs = setup_inputs


def setup_inputs(seed=0):
    import zlib

    import numpy as np

    out = dict(_drawn_inputs(seed))
    spreads = {'L1_ffn_br': (0.0, 0.8), 'L1_ffn_b1': (0.0, 2.0), 'L1_ffn_b2': (0.0, 2.0)}
    factors = {'L1_ffn_Wr': 8.0, 'L1_ffn_W1': 8.0, 'L1_ffn_W2': 8.0}
    for name, (base, spread) in spreads.items():
        noise = np.random.default_rng([zlib.crc32(name.encode()), seed]).standard_normal(out[name].shape)
        drawn = base * np.exp(spread * noise) if base else spread * noise
        out[name] = jnp.asarray(drawn.astype(out[name].dtype))
    for name, factor in factors.items():
        out[name] = (out[name] * factor).astype(out[name].dtype)
    return out
```

```python
import concourse.bass as bass
from concourse import mybir
from contextlib import ExitStack

F32 = mybir.dt.float32
BF16 = mybir.dt.bfloat16
I32 = mybir.dt.int32
U32 = mybir.dt.uint32
ALU = mybir.AluOpType
ACT = mybir.ActivationFunctionType
AX = mybir.AxisListType

B, C, N = 8, 128, 1024
HEADS, DH = 8, 16
G = 2
HG = HEADS // G
P = 128
KT = N // P
HALF = N // 2
TILES = B * KT
QK_SCALE = DH ** -0.5
Q_THRESH, K_THRESH, V_THRESH, MASK_THRESH = 0.25, 0.25, 0.3, 0.1
LN_EPS = 1e-5
E, HID = 8, 512
SLOTS = TILES + E - 1

TERMS = [(0, 0), (0, 1), (1, 0), (1, 1), (0, 2), (2, 0)]
KROWS = DH * len(TERMS)
MROWS = 2
STACK_DMAS = 2 * len(TERMS)


def step_jobs(g, last):
    jobs = []
    nxt = (g + 1) % G
    more = not (last and g == G - 1)
    if more:
        jobs.append((1, "v", (nxt,)))
        if g == 0 and not last:
            jobs += [(14 + 2 * n, "proj", (n // 2, n % 2)) for n in range(4)]
        seq = max_jobs()
        for n, job in enumerate(seq):
            jobs.append((6 + n * 28 // len(seq),) + job)
    jobs += [(40, "sum", (0,)), (40, "sum", (1,))]
    if more:
        jobs += [(42, "mrow", (HG - 1, 0)), (42, "mrow", (HG - 1, 1))]
    if g == G - 1:
        jobs += [(43, "out", (0,)), (43, "out", (1,))]
    return sorted(jobs, key=lambda j: j[0])


def max_jobs():
    seq = []
    for h in range(HG):
        for qt in range(KT):
            for half in range(2):
                seq.append(("max", (h, qt, half)))
            if h and qt == 2:
                seq += [("mrow", (h - 1, 0)), ("mrow", (h - 1, 1))]
    return seq


def body_jobs(last):
    jobs = []
    for g in range(G):
        jobs += [(g,) + j for j in step_jobs(g, last)]
    return jobs


def first_jobs():
    jobs = [("proj", (n // 2, n % 2)) for n in range(4)] + [("v", (0,))] + max_jobs()
    return jobs + [("mrow", (HG - 1, 0)), ("mrow", (HG - 1, 1))]


FIRST = first_jobs()
BODY = body_jobs(False)
LAST = body_jobs(True)
R0, RB = len(FIRST), len(BODY)
assert RB % 2 == 0


def ring(b, off):
    n = R0 + off
    return n % 2, b * (RB // 2) + n // 2


def attention_kernel(nc, sb, psum, sem, x, w_proj, b_proj, w_out, b_out, t_all, ident, identb, parts_dram):
    xp = sb("xp", [P, N], F32)
    xr = sb("xr", [P, N], F32)
    w_qk = [sb(f"w_qk{s}", [C, P], F32) for s in range(2)]
    b_qk = [sb(f"b_qk{s}", [P, 1], F32) for s in range(2)]
    w_v = [sb(f"w_v{g}", [C, HG * DH], F32) for g in range(G)]
    b_v = [sb(f"b_v{g}", [P, HG * DH], F32) for g in range(G)]
    w_o = sb("w_o", [P, G, C], F32)
    b_o = sb("b_o", [P, C], F32)
    spread = sb("spread", [P, P], F32)
    full = [[sb(f"full{s}{h}", [P, HALF], F32) for h in range(2)] for s in range(2)]
    rest = sb("rest", [P, HALF], F32)
    parts = [[sb(f"part{s}{c}", [P, N], BF16) for c in range(3)] for s in range(2)]
    stack = [[sb(f"stack{s}{g}", [P, HG, N], BF16) for g in range(G)] for s in range(2)]
    v_sb = [sb(f"v_sb{g}", [P, KT, HG, 32], F32) for g in range(G)]
    probs = sb("probs", [P, 2, HG, N], F32)
    mx = sb("mx", [P, HG, KT, 2], F32)
    m_all = sb("m_all", [P, KT], F32)
    m_parts = sb("m_parts", [P, HG, KT, MROWS], BF16)
    o_sb = sb("o_sb", [P, 2, HALF], F32)
    o_n = [sb(f"o_n{g}", [P, N], F32) for g in range(G)]

    inv = [sb(f"inv{h}", [P, HALF], F32) for h in range(2)]

    scores = [psum(f"scores{i}", [P, N], F32) for i in range(2)]
    side = [psum(f"side{i}", [P, HALF], F32) for i in range(2)]
    outT = [psum(f"outT{i}", [P, HALF], F32) for i in range(2)]

    s_w = sem("s_w")
    s_xp = sem("s_xp")
    s_xr = sem("s_xr")
    s_const = sem("s_const")
    s_fill = sem("s_fill")
    s_empty = [sem(f"s_empty{i}") for i in range(2)]
    s_proj = sem("s_proj")
    s_split = sem("s_split")
    s_parts = sem("s_parts")
    s_gp = sem("s_gp")
    s_stack = [sem(f"s_stack{g}") for g in range(G)]
    s_mcol = sem("s_mcol")
    s_mm = sem("s_mm")
    s_qk = sem("s_qk")
    s_score_free = sem("s_score_free")
    s_prob_free = sem("s_prob_free")
    s_passed = sem("s_passed")
    s_inv = sem("s_inv")
    s_osb = sem("s_osb")
    block = nc.Block()
    block.__enter__()

    def q_dram(part):
        return w_proj.rearrange("c (h t) -> c h t", t=3 * DH)[:, :, part * DH:(part + 1) * DH]

    @block.sync
    def _(sp):
        sp.dma_start(xp[:, :], x[0]).then_inc(s_xp, 16)
        for s in range(2):
            sp.dma_start(w_qk[s][:, :].rearrange("c (h d) -> c h d", d=DH), q_dram(s)).then_inc(s_w, 16)
            sp.dma_start(b_qk[s][:, :], b_proj.rearrange("(h t d) -> t h d", h=HEADS, t=3)[s].unsqueeze(2)).then_inc(s_w, 16)
        for g in range(G):
            heads = slice(g * HG, (g + 1) * HG)
            sp.dma_start(w_v[g][:, :].rearrange("c (h d) -> c h d", d=DH), q_dram(2)[:, heads, :]).then_inc(s_w, 16)
            sp.dma_start(b_v[g][:, :].rearrange("p (h d) -> p h d", d=DH),
                         b_proj.rearrange("(h t d) -> t h d", h=HEADS, t=3)[2, heads].partition_broadcast(P)
                         ).then_inc(s_w, 16)
        sp.dma_start(b_o[:, :], b_out.partition_broadcast(P)).then_inc(s_w, 16)
        sp.wait_ge(s_const, 1)
        for g in range(G):
            for h in range(HG):
                r = (g * HG + h) * DH
                sp.dma_start(w_o[32 * h:32 * h + DH, g, :], w_out[r:r + DH, :]).then_inc(s_w, 16)
        sp.dma_start(xr[:, :], x[0]).then_inc(s_xr, 16)

        def put_parts():
            for s in range(2):
                for c in range(3):
                    sp.dma_start(parts_dram[s, c], parts[s][c][:, :]).then_inc(s_parts, 16)

        def stack_up(g):
            for n, pair in enumerate(TERMS):
                for s in range(2):
                    src = parts_dram[s, pair[s], g * HG * DH:(g + 1) * HG * DH, :]
                    sp.dma_start(stack[s][g][n * DH:(n + 1) * DH, :, :],
                                 src.rearrange("(h d) n -> d h n", d=DH)).then_inc(s_stack[g], 16)

        sp.wait_ge(s_split, 4)
        put_parts()
        sp.wait_ge(s_parts, 96)
        stack_up(0)

        def batch(b, last):
            sp.wait_ge(s_qk, b * 64 + 1)
            stack_up(1)
            if not last:
                sp.wait_ge(s_fill, b * RB + (R0 + 1))
                sp.dma_start(xp[:, :], x[b + 1]).then_inc(s_xp, 16)
                sp.wait_ge(s_split, b * 4 + 8)
                put_parts()
                sp.wait_ge(s_qk, b * 64 + 32)
                sp.wait_ge(s_parts, b * 96 + 192)
                stack_up(0)
                sp.wait_ge(s_fill, b * RB + (R0 + RB))
                sp.dma_start(xr[:, :], x[b + 1]).then_inc(s_xr, 16)

        with sp.Fori(0, B - 1) as b:
            batch(b, False)
        batch(B - 1, True)

    @block.gpsimd
    def _(pool):
        pool.memset(w_o[:, :, :], 0.0).then_inc(s_const, 1)
        pool.memset(spread[:, :], 0.0).then_inc(s_gp, 1)
        pool.memset(ident[:, :], 0.0).then_inc(s_gp, 1)
        pool.memset(identb[:, :], 0.0).then_inc(s_gp, 1)
        for g in range(G):
            pool.memset(v_sb[g][:, :, :, DH:32], 1.0).then_inc(s_const, 1)
            pool.wait_ge(s_const, 2 * g + 2)
            pool.memset(stack[1][g][KROWS:KROWS + MROWS, :, :], 1.0).then_inc(s_const, 1)
            pool.wait_ge(s_const, 2 * g + 3)
        pool.wait_ge(s_gp, 3)
        pool.affine_select(out=spread[:, :].rearrange("p (j r) -> p j r", r=32),
                           in_=spread[:, :].rearrange("p (j r) -> p j r", r=32),
                           compare_op=ALU.not_equal, fill=1.0, base=-DH,
                           pattern=[[-32, HG], [0, 32]], channel_multiplier=1).then_inc(s_const, 1)
        for m in (ident, identb):
            pool.affine_select(out=m[:, :], in_=m[:, :], compare_op=ALU.not_equal, fill=1.0, base=0,
                               pattern=[[-1, P]], channel_multiplier=1).then_inc(s_const, 1)

        def settled():
            pool.sem_inc(s_passed, 1)

        def split(first, chain):
            for n in range(4):
                s, half = n // 2, n % 2
                cols = slice(half * HALF, (half + 1) * HALF)
                src, part = full[s][half], parts[s]
                pool.wait_ge(s_proj, first + n + 1)
                settled()
                pool.tensor_copy(part[0][:, cols], src[:, :]).then_inc(s_gp, 1)
                pool.wait_ge(s_gp, chain + 4 * n + 1)
                pool.tensor_tensor(rest[:, :], src[:, :], part[0][:, cols], ALU.subtract).then_inc(s_gp, 1)
                pool.wait_ge(s_gp, chain + 4 * n + 2)
                settled()
                pool.tensor_copy(part[1][:, cols], rest[:, :]).then_inc(s_gp, 1)
                pool.wait_ge(s_gp, chain + 4 * n + 3)
                pool.tensor_tensor(part[2][:, cols], rest[:, :], part[1][:, cols], ALU.subtract).then_inc(s_split, 1)
                pool.wait_ge(s_split, first + n + 1)
                pool.sem_inc(s_gp, 1)

        split(0, 3)
        with pool.Fori(0, B - 1) as b:
            pool.wait_ge(s_parts, b * 96 + 96)
            for g in range(G):
                pool.wait_ge(s_stack[g], (b + 1) * (16 * STACK_DMAS))
            split(b * 4 + 4, b * 16 + 19)

    @block.tensor
    def _(pe):
        def side_job(b, off, kind, args, nxt, idx_sum):
            bank, emptied = ring(b, off)
            if not (isinstance(emptied, int) and emptied == 0):
                pe.wait_ge(s_empty[bank], emptied)
            out = side[bank]
            if kind == "proj":
                s, half = args
                mm = pe.matmul(out[:, :], w_qk[s][:, :], xp[:, half * HALF:(half + 1) * HALF], start=True, stop=True)
            elif kind == "v":
                for kt in range(KT):
                    mm = pe.matmul(out[:, kt * 64:(kt + 1) * 64], xp[:, kt * P:(kt + 1) * P], w_v[args[0]][:, :],
                                   start=True, stop=True)
            elif kind == "max":
                h, qt, half = args
                mm = pe.matmul(out[:, :], stack[0][nxt][0:KROWS, h, qt * P:(qt + 1) * P],
                               stack[1][nxt][0:KROWS, h, half * HALF:(half + 1) * HALF], start=True, stop=True)
            elif kind == "mrow":
                h, half = args
                for q in range(KT // 2):
                    mm = pe.matmul(out[KROWS:KROWS + MROWS, q * P:(q + 1) * P],
                                   m_parts[:, h, half * (KT // 2) + q, :], identb[:, :], start=True, stop=True)
            elif kind == "sum":
                mm = pe.matmul(out[:, :], spread[:, :], o_sb[:, args[0], :], start=True, stop=True)
            elif kind == "out":
                j = args[0]
                for q in range(KT // 2):
                    tok = slice((j * (KT // 2) + q) * P, (j * (KT // 2) + q + 1) * P)
                    dst = out[:, q * C:(q + 1) * C]
                    pe.matmul(dst, o_n[0][:, tok], w_o[:, 0, :], start=True, stop=False)
                    pe.matmul(dst, o_n[1][:, tok], w_o[:, 1, :], start=False, stop=False)
                    mm = pe.matmul(dst, xr[:, tok], ident[:, :], start=False, stop=True)
            mm.then_inc(s_fill, 1)

        pe.sem_inc(s_score_free, 2)
        pe.sem_inc(s_prob_free, 2)
        pe.sem_inc(s_osb, 1)
        pe.wait_ge(s_w, 16 * (4 + 2 * G + 1 + HEADS))
        pe.wait_ge(s_xp, 16)
        pe.wait_ge(s_const, 2 + 2 * G + 2)
        first_max = True
        for n, (kind, args) in enumerate(FIRST):
            if kind == "max" and first_max:
                pe.wait_ge(s_stack[0], 16 * STACK_DMAS)
                first_max = False
            if kind == "mrow" and args[1] == 0:
                pe.wait_ge(s_mm, args[0] + 1)
            side_job(0, n - R0, kind, args, 0, None)

        def scores_v(b, g, kt):
            if kt == 0:
                pe.wait_ge(s_osb, b * 2 + (g + 1))
            pe.wait_ge(s_score_free, b * 64 + (2 + 32 * g + 4 * kt + 4))
            for half in range(2):
                for h in range(HG):
                    mm = pe.matmul(outT[half][32 * h:32 * h + 32, :], v_sb[g][:, kt, h, :],
                                   probs[:, kt % 2, h, half * HALF:(half + 1) * HALF],
                                   start=(kt == 0), stop=(kt == KT - 1))
            mm.then_inc(s_prob_free, 1)

        def batch(b, jobs, last):
            off = 0
            for g in range(G):
                nxt = (g + 1) % G
                todo = [j for j in jobs if j[0] == g]
                for back in (1, 2):
                    bank, emptied = ring(b, off - back)
                    pe.wait_ge(s_empty[bank], emptied + 1)
                started = False
                for i in range(32 + 12):
                    if i < 32:
                        kt, h = i // HG, i % HG
                        pe.wait_ge(s_score_free, b * 64 + (32 * g + i + 1))
                        for half in range(2):
                            mm = pe.matmul(scores[i % 2][:, half * HALF:(half + 1) * HALF],
                                           stack[1][g][0:KROWS + MROWS, h, kt * P:(kt + 1) * P],
                                           stack[0][g][0:KROWS + MROWS, h, half * HALF:(half + 1) * HALF],
                                           start=True, stop=True)
                        mm.then_inc(s_qk, 1)
                    if i % 4 == 1 and 5 <= i <= 33:
                        scores_v(b, g, (i - 5) // 4)
                    while todo and todo[0][1] <= i:
                        _, _, kind, args = todo.pop(0)
                        if kind == "max" and not started:
                            pe.wait_ge(s_stack[nxt], (b + (1 + g)) * (16 * STACK_DMAS))
                            started = True
                        if kind == "v" and g == 1 and not last:
                            pe.wait_ge(s_xp, b * 16 + 32)
                        if kind == "proj":
                            pe.wait_ge(s_xp, b * 16 + 32)
                        if kind == "mrow" and args[1] == 0:
                            pe.wait_ge(s_mm, b * 8 + (4 * g + 4 + args[0] + 1))
                        if kind == "sum" and args[0] == 0:
                            pe.wait_ge(s_osb, b * 2 + (g + 2))
                        if kind == "out":
                            pe.wait_ge(s_xr, b * 16 + 16)
                        side_job(b, off, kind, args, nxt, None)
                        off += 1

        with pe.Fori(0, B - 1) as b:
            batch(b, BODY, False)
        batch(B - 1, LAST, True)

    @block.scalar
    def _(act):
        def maximum_row(b, off, nxt, args):
            h, half = args
            bank, emptied = ring(b, off)
            act.wait_ge(s_fill, b * RB + (R0 + off + 1))
            act.activation(stack[0][nxt][KROWS:KROWS + MROWS, h, half * HALF:(half + 1) * HALF],
                           side[bank][KROWS:KROWS + MROWS, :], ACT.Copy).then_inc(s_empty[bank], 1)

        for n, (kind, args) in enumerate(FIRST):
            if kind == "mrow":
                maximum_row(0, n - R0, 0, args)

        def batch(b, jobs):
            off = 0
            for g in range(G):
                todo = [j for j in jobs if j[0] == g]
                for i in range(32 + 12):
                    if i < 32:
                        kt, h = i // HG, i % HG
                        if h == 0:
                            act.wait_ge(s_prob_free, b * 16 + (8 * g + kt + 1))
                        act.wait_ge(s_qk, b * 64 + (32 * g + i + 1))
                        act.activation(probs[:, kt % 2, h, :], scores[i % 2][:, :], ACT.Exp).then_inc(s_score_free, 1)
                    if i == 34:
                        act.wait_ge(s_prob_free, b * 16 + (2 + 8 * g + KT))
                        act.activation(o_sb[:, 0, :], outT[0][:, :], ACT.Copy)
                        act.activation(o_sb[:, 1, :], outT[1][:, :], ACT.Copy).then_inc(s_osb, 1)
                    while todo and todo[0][1] <= i:
                        _, _, kind, args = todo.pop(0)
                        if kind == "mrow":
                            maximum_row(b, off, (g + 1) % G, args)
                        off += 1

        with act.Fori(0, B - 1) as b:
            batch(b, BODY)
        batch(B - 1, LAST)

    @block.vector
    def _(dve):
        def side_job(b, off, kind, args, nxt, g, steps):
            bank, emptied = ring(b, off)
            if kind == "mrow":
                return
            dve.wait_ge(s_fill, b * RB + (R0 + off + 1))
            ps = side[bank]
            if kind == "proj":
                s, half = args
                if steps is not None:
                    dve.wait_ge(s_split, b * 4 + 4)
                dve.tensor_scalar(full[s][half][:, :], ps[:, :], b_qk[s][:, 0:1], QK_SCALE if s == 0 else 1.0,
                                  ALU.add, ALU.mult).then_inc(s_empty[bank], 1)
                dve.wait_ge(s_empty[bank], emptied + 1)
                dve.sem_inc(s_proj, 1)
            elif kind == "v":
                gg = args[0]
                dve.tensor_tensor(v_sb[gg][:, :, :, 0:DH],
                                  ps[:, :].rearrange("p (k h d) -> p k h d", k=KT, d=DH),
                                  b_v[gg][:, :].rearrange("p (h d) -> p h d", d=DH).unsqueeze(1)
                                  .broadcast_to([P, KT, HG, DH]), ALU.add).then_inc(s_empty[bank], 1)
            elif kind == "max":
                h, qt, half = args
                dve.tensor_reduce(mx[:, h, qt, half:half + 1], ps[:, :], AX.X, ALU.max).then_inc(s_empty[bank], 1)
                if qt == KT - 1 and half == 1:
                    done = h if steps is None else steps + h
                    dve.wait_ge(s_empty[bank], emptied + 1)
                    bank2, emptied2 = ring(b, off - 1)
                    dve.wait_ge(s_empty[bank2], emptied2 + 1)
                    dve.tensor_reduce(m_all[:, :], mx[:, h, :, :], AX.X, ALU.max).then_inc(s_mcol, 1)
                    dve.wait_ge(s_mcol, done * 2 + 1)
                    dve.tensor_scalar(m_parts[:, h, :, 0], m_all[:, :], -1.0, None, ALU.mult).then_inc(s_mcol, 1)
                    dve.wait_ge(s_mcol, done * 2 + 2)
                    dve.scalar_tensor_tensor(out=m_parts[:, h, :, 1], in0=m_all[:, :], scalar=-1.0,
                                             in1=m_parts[:, h, :, 0], op0=ALU.mult, op1=ALU.subtract).then_inc(s_mm, 1)
                    dve.wait_ge(s_mm, done + 1)
            elif kind == "sum":
                half = args[0]
                before = b * 4 + (2 * g + half)
                dve.reciprocal(inv[half][:, :], ps[:, :]).then_inc(s_inv, 1)
                dve.wait_ge(s_inv, before + 1)
                dve.tensor_tensor(o_n[g][:, half * HALF:(half + 1) * HALF], o_sb[:, half, :], inv[half][:, :],
                                  ALU.mult).then_inc(s_empty[bank], 1)
            elif kind == "out":
                first = b * KT + args[0] * (KT // 2)
                dve.tensor_tensor(t_all[:, bass.ds(first, KT // 2), :], ps[:, :].rearrange("p (q c) -> p q c", c=C),
                                  b_o[:, :].unsqueeze(1).broadcast_to([P, KT // 2, C]),
                                  ALU.add).then_inc(s_empty[bank], 1)

        dve.wait_ge(s_w, 16 * (4 + 2 * G + 1 + HEADS))
        dve.wait_ge(s_const, 2 + 2 * G + 2)
        for n, (kind, args) in enumerate(FIRST):
            side_job(0, n - R0, kind, args, 0, 0, None)

        def batch(b, jobs):
            for off, (g, slot, kind, args) in enumerate(jobs):
                side_job(b, off, kind, args, (g + 1) % G, g, b * 8 + 4 * (g + 1))

        with dve.Fori(0, B - 1) as b:
            batch(b, BODY)
        batch(B - 1, LAST)

    block.__exit__(None, None, None)


def tile_of(ap, n):
    return ap[:, bass.ds(n, 1), :].rearrange("p a s -> p (a s)")


def token_statistics(nc, sb, sem, t_all, tag):
    stats = sb(f"stats{tag}", [P, TILES, 6], F32)
    mv = sb(f"mv{tag}", [P, TILES, 2], F32)
    std = sb(f"std{tag}", [P, TILES], F32)
    rstd = sb(f"rstd{tag}", [P, TILES], F32)
    s_stat = sem(f"s_stat{tag}")
    s_std = sem(f"s_std{tag}")
    with nc.Block() as block:
        @block.vector
        def _(dve):
            with dve.Fori(0, B) as b:
                for k in range(KT):
                    dve.bn_stats(tile_of(stats, b * KT + k), tile_of(t_all, b * KT + k)).then_inc(s_stat, 1)
            dve.wait_ge(s_stat, TILES)
            for k in range(TILES):
                last = dve.bn_aggr(mv[:, k, :], stats[:, k, :])
            last.then_inc(s_stat, 1)
            dve.wait_ge(s_stat, TILES + 1)
            dve.tensor_scalar(std[:, :], mv[:, :, 1], LN_EPS, None, ALU.add).then_inc(s_stat, 1)
            dve.wait_ge(s_std, 1)
            dve.reciprocal(rstd[:, :], std[:, :])

        @block.scalar
        def _(act):
            act.wait_ge(s_stat, TILES + 2)
            act.activation(std[:, :], std[:, :], ACT.Sqrt).then_inc(s_std, 1)
    return mv, rstd


def normalise(eng, out, t_all, mv, rstd, n):
    return eng.tensor_scalar(out, tile_of(t_all, n), mv[:, bass.ds(n, 1), 0], rstd[:, bass.ds(n, 1)],
                             ALU.subtract, ALU.mult)


BANKS = 8
MASKS = [(m, lo, min(lo + HALF, N)) for m in range(KT) for lo in range(m * P, N, HALF)]
TURN_SPIKE = [("turn", (j,)) for j in range(2)] + [("spike", (s, half)) for s in range(2) for half in range(2)]
SPIKE_V = [("spike_v", (j,)) for j in range(2)]
COUNT = [("count", (j,)) for j in range(4)]
MASK = [("mask", m) for m in MASKS]
SPIKE_FIRST = TURN_SPIKE + SPIKE_V
SPIKE_BODY = MASK + TURN_SPIKE + COUNT + SPIKE_V
SPIKE_LAST = MASK + COUNT
assert len(SPIKE_FIRST) == BANKS and len(SPIKE_BODY) % BANKS == 0


def spike_use(b, n):
    return n % BANKS, b * (len(SPIKE_BODY) // BANKS) + (BANKS + n) // BANKS


def spike_kernel(nc, sb, psum, sem, wq, wk, wv, t_all, mv, rstd, ident, rows_in):
    w_raw = sb("w_raw", [P, 3, C], F32)
    w_t = sb("w_t", [P, 3, C], F32)
    zeros = sb("zeros", [P, C], F32)
    z = sb("z", [P, KT, C], F32)
    zt = sb("zt", [P, N], F32)
    spikes = [sb(f"spikes{s}", [P, N], BF16) for s in range(2)]
    spikes_v = sb("spikes_v", [P, KT, C], BF16)
    mask = sb("mask", [P, KT, N], BF16)
    causal = sb("causal", [P, P], BF16)
    bank = [psum(f"bank{i}", [P, HALF], F32) for i in range(BANKS)]
    s_w = sem("sp_w")
    s_c = sem("sp_c")
    s_wt = sem("sp_wt")
    s_wc = sem("sp_wc")
    s_z = sem("sp_z")
    s_fill = sem("sp_fill")
    s_zero = sem("sp_zero")
    s_empty = [sem(f"sp_empty{i}") for i in range(BANKS)]

    with nc.Block() as block:
        @block.sync
        def _(sp):
            for n, w in enumerate((wq, wk, wv)):
                sp.dma_start(w_raw[:, n, :], w).then_inc(s_w, 16)
            sp.wait_ge(s_c, 3)
            sp.dma_start(rows_in.rearrange("(s p) c -> p s c", p=P),
                         zeros[:, :].unsqueeze(1).broadcast_to([P, SLOTS + 1, C])).then_inc(s_zero, 16)
            sp.wait_ge(s_zero, 16)

        @block.gpsimd
        def _(pool):
            pool.memset(causal[:, :], 1.0).then_inc(s_c, 1)
            pool.wait_ge(s_c, 1)
            pool.affine_select(out=causal[:, :], in_=causal[:, :], compare_op=ALU.is_ge, fill=0.0, base=0,
                               pattern=[[1, P]], channel_multiplier=-1).then_inc(s_c, 1)
            pool.memset(zeros[:, :], 0.0).then_inc(s_c, 1)

        @block.tensor
        def _(pe):
            pe.wait_ge(s_w, 48)
            for n in range(3):
                mm = pe.transpose(bank[0][:, n * C:(n + 1) * C], w_raw[:, n, :], ident[:, :])
            mm.then_inc(s_wt, 1)
            pe.wait_ge(s_wc, 1)

            def use(b, n, kind, args, tiles):
                i, emptied = spike_use(b, n)
                out = bank[i]
                if kind == "mask" and args[0] == 0 and args[1] == 0:
                    for back in range(1, BANKS + 1):
                        j, before = spike_use(b, n - back)
                        pe.wait_ge(s_empty[j], before + 1)
                elif kind == "count" and args[0] == 0:
                    for m in range(n - BANKS, len(MASKS)):
                        j, before = spike_use(b, m)
                        pe.wait_ge(s_empty[j], before + 1)
                elif b is not None and not (n < 0):
                    pe.wait_ge(s_empty[i], emptied)
                if kind == "turn":
                    pe.wait_ge(s_z, tiles)
                    for q in range(4):
                        mm = pe.transpose(out[:, q * P:(q + 1) * P], z[:, args[0] * 4 + q, :], ident[:, :])
                elif kind == "spike":
                    s, half = args
                    if s == 0:
                        j, before = spike_use(b, n - 2)
                        pe.wait_ge(s_empty[j], before + 1)
                    mm = pe.matmul(out[:, :], w_t[:, s, :], zt[:, half * HALF:(half + 1) * HALF], start=True, stop=True)
                elif kind == "spike_v":
                    for q in range(4):
                        tok = args[0] * 4 + q
                        mm = pe.matmul(out[:, q * C:(q + 1) * C], zt[:, tok * P:(tok + 1) * P], w_t[:, 2, :],
                                       start=True, stop=True)
                elif kind == "mask":
                    m, lo, hi = args
                    mm = pe.matmul(out[:, 0:hi - lo], spikes[1][:, m * P:(m + 1) * P], spikes[0][:, lo:hi],
                                   start=True, stop=True)
                elif kind == "count":
                    for q in range(2):
                        l = args[0] * 2 + q
                        for m in range(l + 1):
                            mm = pe.matmul(out[:, q * C:(q + 1) * C], mask[:, m, l * P:(l + 1) * P],
                                           spikes_v[:, m, :], start=(m == 0), stop=(m == l))
                mm.then_inc(s_fill, 1)

            for n, (kind, args) in enumerate(SPIKE_FIRST):
                use(0, n - BANKS, kind, args, KT)
            with pe.Fori(0, B - 1) as b:
                for n, (kind, args) in enumerate(SPIKE_BODY):
                    use(b, n, kind, args, b * KT + 2 * KT)
            for n, (kind, args) in enumerate(SPIKE_LAST):
                use(B - 1, n, kind, args, 0)

        @block.scalar
        def _(act):
            act.wait_ge(s_wt, 1)
            act.activation(w_t[:, :, :], bank[0][:, 0:3 * C].rearrange("p (n c) -> p n c", n=3),
                           ACT.Copy).then_inc(s_wc, 1)

            def turned(b, n, j):
                i, _ = spike_use(b, n)
                act.wait_ge(s_fill, b * len(SPIKE_BODY) + (BANKS + n + 1))
                act.activation(zt[:, j * HALF:(j + 1) * HALF], bank[i][:, :], ACT.Copy).then_inc(s_empty[i], 1)

            for j in range(2):
                turned(0, j - BANKS, j)
            with act.Fori(0, B - 1) as b:
                for j in range(2):
                    turned(b, len(MASKS) + j, j)

        @block.vector
        def _(dve):
            def normalise_batch(b):
                for k in range(KT):
                    normalise(dve, z[:, k, :], t_all, mv, rstd, b * KT + k).then_inc(s_z, 1)

            def use(b, n, kind, args):
                i, emptied = spike_use(b, n)
                if kind == "turn":
                    return
                dve.wait_ge(s_fill, b * len(SPIKE_BODY) + (BANKS + n + 1))
                ps = bank[i]
                if kind == "spike":
                    s, half = args
                    dve.tensor_scalar(spikes[s][:, half * HALF:(half + 1) * HALF], ps[:, :], (Q_THRESH, K_THRESH)[s],
                                      None, ALU.is_ge).then_inc(s_empty[i], 1)
                elif kind == "spike_v":
                    dve.tensor_scalar(spikes_v[:, args[0] * 4:args[0] * 4 + 4, :],
                                      ps[:, :].rearrange("p (q c) -> p q c", c=C), V_THRESH, None,
                                      ALU.is_ge).then_inc(s_empty[i], 1)
                elif kind == "mask":
                    m, lo, hi = args
                    at = lo
                    if lo == m * P:
                        last = dve.scalar_tensor_tensor(out=mask[:, m, lo:lo + P], in0=ps[:, 0:P], scalar=MASK_THRESH,
                                                        in1=causal[:, :], op0=ALU.is_gt, op1=ALU.mult)
                        at = lo + P
                    if at < hi:
                        last = dve.tensor_scalar(mask[:, m, at:hi], ps[:, at - lo:hi - lo], MASK_THRESH, None, ALU.is_gt)
                    last.then_inc(s_empty[i], 1)
                elif kind == "count":
                    tiles = t_all[:, bass.ds(b * KT + args[0] * 2, 2), :]
                    dve.tensor_tensor(tiles, tiles, ps[:, 0:2 * C].rearrange("p (q c) -> p q c", c=C),
                                      ALU.add).then_inc(s_empty[i], 1)

            dve.wait_ge(s_c, 3)
            normalise_batch(0)
            for n, (kind, args) in enumerate(SPIKE_FIRST):
                use(0, n - BANKS, kind, args)
            with dve.Fori(0, B - 1) as b:
                normalise_batch(b + 1)
                for n, (kind, args) in enumerate(SPIKE_BODY):
                    use(b, n, kind, args)
            for n, (kind, args) in enumerate(SPIKE_LAST):
                use(B - 1, n, kind, args)


def routing_kernel(nc, sb, psum, sem, wr, br, t_all, z_all, mv, rstd, ident, pos, slot_expert, gain):
    w_r = sb("w_r", [P, E], F32)
    b_r = sb("b_r", [P, E], F32)
    zt = sb("r_zt", [P, 2, HALF], F32)
    before = sb("before", [P, P], BF16)
    ones = sb("ones", [P, P], BF16)
    rank = sb("rank", [P, E], F32)
    slot_no = sb("slot_no", [P, SLOTS], F32)
    logit = sb("logit", [P, TILES, E], F32)
    prob = sb("prob", [P, TILES, E], F32)
    work = sb("work", [P, TILES, E], F32)
    chosen = sb("chosen", [P, TILES, E], BF16)
    col = [sb(f"col{i}", [P, TILES], F32) for i in range(6)]
    keep = sb("keep", [P, E, TILES], F32)
    count = sb("count", [P, E, TILES], F32)
    upto = sb("upto", [P, E, TILES], F32)
    total = sb("total", [P, E], F32)
    total_i = sb("total_i", [P, E], I32)
    tiles_i = sb("tiles_i", [P, E], I32)
    tiles_e = sb("tiles_e", [P, E], F32)
    end_e = sb("end_e", [P, E], F32)
    base_e = sb("base_e", [P, E], F32)
    ones_e = sb("ones_e", [P, E], F32)
    past = sb("past", [P, SLOTS, E], F32)
    slot_f = sb("slot_f", [P, SLOTS], F32)
    ps_t = [psum(f"r_turn{i}", [P, HALF], F32) for i in range(2)]
    ps_logit = psum("ps_logit", [P, TILES * E], F32)
    ps_before = psum("ps_before", [P, TILES * E], F32)
    ps_count = psum("ps_count", [P, TILES * E], F32)
    s_w = sem("r_w")
    s_c = sem("r_c")
    s_z = sem("r_z")
    s_turn = sem("r_turn")
    s_zt = sem("r_zt")
    s_logit = sem("r_logit")
    s_shift = sem("r_shift")
    s_exp = sem("r_exp")
    s_chosen = sem("r_chosen")
    s_sum = sem("r_sum")
    s_v = sem("r_v")
    DVE_CONST = 2

    with nc.Block() as block:
        @block.sync
        def _(sp):
            sp.dma_start(w_r[:, :], wr).then_inc(s_w, 16)
            sp.dma_start(b_r[:, :], br.partition_broadcast(P)).then_inc(s_w, 16)

        @block.gpsimd
        def _(pool):
            pool.memset(before[:, :], 1.0).then_inc(s_c, 1)
            pool.memset(ones[:, :], 1.0).then_inc(s_c, 1)
            pool.memset(ones_e[:, :], 1.0).then_inc(s_c, 1)
            pool.memset(keep[:, :, 1:TILES], 1.0).then_inc(s_c, 1)
            pool.memset(keep[:, :, 0:1], 0.0).then_inc(s_c, 1)
            pool.iota(rank[:, :], [[-1, E]], base=E, channel_multiplier=0,
                      allow_small_or_imprecise_dtypes=True).then_inc(s_c, 1)
            pool.iota(slot_no[:, :], [[1, SLOTS]], base=0, channel_multiplier=0,
                      allow_small_or_imprecise_dtypes=True).then_inc(s_c, 1)
            pool.wait_ge(s_c, 7)
            pool.affine_select(out=before[:, :], in_=before[:, :], compare_op=ALU.is_gt, fill=0.0, base=0,
                               pattern=[[1, P]], channel_multiplier=-1).then_inc(s_c, 1)

        @block.tensor
        def _(pe):
            pe.wait_ge(s_w, 32)
            for b in range(B):
                pe.wait_ge(s_z, b * KT + KT)
                for j in range(2):
                    for q in range(4):
                        mm = pe.transpose(ps_t[j][:, q * P:(q + 1) * P], z_all[:, b * KT + 4 * j + q, :], ident[:, :])
                    mm.then_inc(s_turn, 1)
                for j in range(2):
                    pe.wait_ge(s_zt, b * 2 + (j + 1))
                    for q in range(4):
                        t = b * KT + 4 * j + q
                        mm = pe.matmul(ps_logit[:, t * E:(t + 1) * E], zt[:, j, q * P:(q + 1) * P], w_r[:, :],
                                       start=True, stop=True)
                mm.then_inc(s_logit, 1)
            pe.wait_ge(s_chosen, 1)
            pe.wait_ge(s_c, 8)
            flat = chosen[:, :, :].rearrange("p t e -> p (t e)")
            pe.matmul(ps_before[:, :], before[:, :], flat, start=True, stop=True).then_inc(s_sum, 1)
            pe.matmul(ps_count[:, :], ones[:, :], flat, start=True, stop=True).then_inc(s_sum, 1)

        @block.scalar
        def _(act):
            with act.Fori(0, B) as b:
                for j in range(2):
                    act.wait_ge(s_turn, b * 2 + (j + 1))
                    act.activation(zt[:, j, :], ps_t[j][:, :], ACT.Copy).then_inc(s_zt, 1)
            act.wait_ge(s_shift, 1)
            act.activation(prob[:, :, :], logit[:, :, :], ACT.Exp).then_inc(s_exp, 1)

        @block.vector
        def _(dve):
            steps = [0]

            def step(instruction):
                steps[0] += 1
                instruction.then_inc(s_v, 1)
                dve.wait_ge(s_v, steps[0])

            def over_e(column):
                return column.unsqueeze(2).broadcast_to([P, TILES, E])

            with dve.Fori(0, B) as b:
                for k in range(KT):
                    normalise(dve, tile_of(z_all, b * KT + k), t_all, mv, rstd, b * KT + k).then_inc(s_z, 1)
            dve.wait_ge(s_w, 32)
            dve.wait_ge(s_c, 8)
            dve.wait_ge(s_logit, B)
            step(dve.tensor_tensor(work[:, :, :], ps_logit[:, :].rearrange("p (t e) -> p t e", e=E),
                                   b_r[:, :].unsqueeze(1).broadcast_to([P, TILES, E]), ALU.add))
            step(dve.tensor_reduce(col[0][:, :], work[:, :, :], AX.X, ALU.max))
            dve.tensor_tensor(logit[:, :, :], work[:, :, :], over_e(col[0][:, :]), ALU.subtract).then_inc(s_shift, 1)
            dve.wait_ge(s_exp, 1)
            step(dve.tensor_reduce(col[1][:, :], prob[:, :, :], AX.X, ALU.add))
            step(dve.reciprocal(col[2][:, :], col[1][:, :]))
            step(dve.tensor_tensor(work[:, :, :], prob[:, :, :], over_e(col[2][:, :]), ALU.mult))
            step(dve.tensor_reduce(col[3][:, :], work[:, :, :], AX.X, ALU.max))
            step(dve.reciprocal(col[4][:, :], col[3][:, :]))
            step(dve.tensor_tensor(gain[:, :], col[3][:, :], col[4][:, :], ALU.mult))
            step(dve.tensor_tensor(prob[:, :, :], work[:, :, :], over_e(col[3][:, :]), ALU.is_ge))
            step(dve.tensor_tensor(work[:, :, :], prob[:, :, :], rank[:, :].unsqueeze(1).broadcast_to([P, TILES, E]),
                                   ALU.mult))
            step(dve.tensor_reduce(col[5][:, :], work[:, :, :], AX.X, ALU.max))
            dve.tensor_tensor(chosen[:, :, :], work[:, :, :], over_e(col[5][:, :]), ALU.is_ge).then_inc(s_chosen, 1)
            dve.wait_ge(s_sum, 2)
            step(dve.tensor_copy(count[:, :, :], ps_count[:, :].rearrange("p (t e) -> p e t", e=E)))
            step(dve.tensor_tensor_scan(upto[:, :, :].rearrange("p e t -> p (e t)"),
                                        keep[:, :, :].rearrange("p e t -> p (e t)"),
                                        count[:, :, :].rearrange("p e t -> p (e t)"), 0.0, ALU.mult, ALU.add))
            step(dve.tensor_scalar(total_i[:, :], upto[:, :, TILES - 1], float(P - 1), None, ALU.add))
            step(dve.tensor_scalar(tiles_i[:, :], total_i[:, :], 7, None, ALU.arith_shift_right))
            step(dve.tensor_copy(tiles_e[:, :], tiles_i[:, :]))
            step(dve.tensor_tensor_scan(end_e[:, :], ones_e[:, :], tiles_e[:, :], 0.0, ALU.mult, ALU.add))
            step(dve.tensor_tensor(total[:, :], end_e[:, :], tiles_e[:, :], ALU.subtract))
            step(dve.tensor_scalar(base_e[:, :], total[:, :], float(P), None, ALU.mult))
            step(dve.tensor_tensor(upto[:, :, :], upto[:, :, :], count[:, :, :], ALU.subtract))
            step(dve.tensor_tensor(count[:, :, :], upto[:, :, :], base_e[:, :].unsqueeze(2).broadcast_to([P, E, TILES]),
                                   ALU.add))
            step(dve.tensor_tensor(upto[:, :, :], count[:, :, :], ps_before[:, :].rearrange("p (t e) -> p e t", e=E),
                                   ALU.add))
            step(dve.tensor_tensor(work[:, :, :], upto[:, :, :].rearrange("p e t -> p t e"), chosen[:, :, :], ALU.mult))
            step(dve.tensor_reduce(col[0][:, :], work[:, :, :], AX.X, ALU.add))
            step(dve.tensor_copy(pos[:, :], col[0][:, :]))
            step(dve.tensor_tensor(past[:, :, :], slot_no[:, :].unsqueeze(2).broadcast_to([P, SLOTS, E]),
                                   end_e[:, :].unsqueeze(1).broadcast_to([P, SLOTS, E]), ALU.is_ge))
            step(dve.tensor_reduce(slot_f[:, :], past[:, :, :], AX.X, ALU.add))
            step(dve.tensor_scalar(slot_expert[:, :], slot_f[:, :], float(E - 1), None, ALU.min))


def expert_kernel(nc, sb, psum, sem, w1, b1, w2, b2, z_all, t_all, ident, pos, slot_expert, gain, rows_in, rows_out, out):
    HC = HID // P
    w1_sb = sb("w1_sb", [P, E, HID], F32)
    w2_sb = sb("w2_sb", [P, E, HC, C], F32)
    b1_sb = sb("b1_sb", [P, E, HID], F32)
    b2_sb = sb("b2_sb", [P, E, C], F32)
    RING = 4
    x_in = sb("x_in", [P, RING, C], F32)
    xt = sb("xt", [P, 2, P], F32)
    hid_b = sb("hid_b", [P, 2, HID], F32)
    hid = sb("hid", [P, 2, HID], F32)
    hid_t = sb("hid_t", [P, 2, HID], F32)
    y = sb("y", [P, RING, C], F32)
    out_t = sb("out_t", [P, 2, HALF], F32)
    ps_x = [psum(f"ps_x{i}", [P, HALF], F32) for i in range(2)]
    ps_h = [psum(f"ps_h{i}", [P, HALF], F32) for i in range(2)]
    ps_t = [psum(f"ps_t{i}", [P, HALF], F32) for i in range(2)]
    ps_y = [psum(f"ps_y{i}", [P, HALF], F32) for i in range(2)]
    s_w = sem("e_w")
    s_sent = sem("e_sent")
    s_x = [sem(f"e_x{i}") for i in range(RING)]
    s_turn = sem("e_turn")
    s_xt = sem("e_xt")
    s_up = sem("e_up")
    s_bias = sem("e_bias")
    s_gelu = sem("e_gelu")
    s_ht = sem("e_ht")
    s_htc = sem("e_htc")
    s_down = sem("e_down")
    s_y = sem("e_y")
    s_st = [sem(f"e_st{i}") for i in range(RING)]
    s_back = [sem(f"e_back{i}") for i in range(B)]
    s_gain = sem("e_gain")
    s_add = sem("e_add")
    s_ot = sem("e_ot")
    s_oc = sem("e_oc")
    s_out = [sem(f"e_out{i}") for i in range(2)]
    AHEAD = 3
    assert (SLOTS - AHEAD) % RING == 0

    def slots(eng, f):
        for s in range(1, AHEAD):
            f(s, s, s)
        with eng.Fori(0, (SLOTS - AHEAD) // RING) as i:
            for j in range(RING):
                f(i * RING + (AHEAD + j), AHEAD + j, i)

    def rounds(i, n):
        return i + n // RING

    with nc.Block() as block:
        @block.sync
        def _(sp):
            sp.dma_start(w1_sb[:, :, :], w1.rearrange("e c h -> c e h")).then_inc(s_w, 16)
            sp.dma_start(w2_sb[:, :, :, :], w2.rearrange("e (k p) c -> p e k c", p=P)).then_inc(s_w, 16)
            sp.dma_start(b1_sb[:, :, :], b1.partition_broadcast(P)).then_inc(s_w, 16)
            sp.dma_start(b2_sb[:, :, :], b2.partition_broadcast(P)).then_inc(s_w, 16)

            def row(s):
                return s * P if isinstance(s, int) else sp.snap(s * P)

            def load(s, r, turned=None):
                first = row(s)
                if turned is not None:
                    sp.wait_ge(s_turn, turned)
                sp.dma_start(x_in[:, r, :], rows_in[bass.ds(first, P), :]).then_inc(s_x[r], 16)

            def store(s, r):
                first = row(s)
                sp.wait_ge(s_y, s + 1)
                sp.dma_start(rows_out[bass.ds(first, P), :], y[:, r, :]).then_inc(s_st[r], 16)

            sp.wait_ge(s_sent, 16 * TILES)
            for s in range(RING):
                load(s, s)

            for s in range(1, AHEAD):
                load(s + 3, (s + 3) % RING, s)
                store(s - 1, s - 1)
            with sp.Fori(0, (SLOTS - AHEAD) // RING - 1) as i:
                for j in range(RING):
                    n = AHEAD + j
                    load(i * RING + (n + 3), (n + 3) % RING, i * RING + n)
                    store(i * RING + (n - 1), (n - 1) % RING)
            for s in range(SLOTS - RING, SLOTS):
                if s + 3 <= SLOTS:
                    load(s + 3, (s + 3) % RING, s)
                store(s - 1, (s - 1) % RING)
            store(SLOTS - 1, (SLOTS - 1) % RING)

            for b in range(B):
                for j in range(2):
                    sp.wait_ge(s_oc, 2 * b + j + 1)
                    sp.dma_start(out[b, :, j * HALF:(j + 1) * HALF], out_t[:, j, :]).then_inc(s_out[j], 16)
            for j in range(2):
                sp.wait_ge(s_out[j], 16 * B)

        @block.gpsimd
        def _(pool):
            for t in range(TILES):
                pool.indirect_dma_start(rows_in, bass.IndirectOffsetOnAxis(ap=pos[:, t:t + 1], axis=0),
                                        z_all[:, t, :], None).then_inc(s_sent, 16)
            for r in range(RING):
                pool.wait_ge(s_st[r], 16 * len(range(r, SLOTS, RING)))
            pool.wait_ge(s_sent, 16 * TILES)
            for t in range(TILES):
                pool.indirect_dma_start(z_all[:, t, :], None, rows_out,
                                        bass.IndirectOffsetOnAxis(ap=pos[:, t:t + 1], axis=0)).then_inc(s_back[t // KT], 16)

        @block.tensor
        def _(pe):
            def turn(s, n, i):
                pe.wait_ge(s_x[n % RING], rounds(i, n) * 16 + 16)
                if n >= 2:
                    pe.wait_ge(s_xt, s - 1)
                pe.transpose(ps_x[n % 2][:, 0:P], x_in[:, n % RING, :], ident[:, :]).then_inc(s_turn, 1)

            def up(s, n):
                e = pe.value_load(slot_expert[0:1, bass.ds(s, 1)], min_val=0, max_val=E - 1)
                pe.wait_ge(s_xt, s + 1)
                if n >= 2:
                    pe.wait_ge(s_bias, s - 1)
                pe.matmul(ps_h[n % 2][:, :], xt[:, n % 2, :], tile_of(w1_sb, e), start=True, stop=True).then_inc(s_up, 1)
                return e

            def hidden_turn(s, n):
                pe.wait_ge(s_gelu, s + 1)
                if n >= 2:
                    pe.wait_ge(s_htc, s - 1)
                for k in range(HC):
                    mm = pe.transpose(ps_t[n % 2][:, k * P:(k + 1) * P], hid[:, n % 2, k * P:(k + 1) * P], ident[:, :])
                mm.then_inc(s_ht, 1)

            def down(s, n, e):
                pe.wait_ge(s_htc, s + 1)
                if n >= 2:
                    pe.wait_ge(s_y, s - 1)
                w = w2_sb[:, bass.ds(e, 1), :, :].rearrange("p a k c -> p (a k) c")
                for k in range(HC):
                    mm = pe.matmul(ps_y[n % 2][:, 0:C], hid_t[:, n % 2, k * P:(k + 1) * P], w[:, k, :],
                                   start=(k == 0), stop=(k == HC - 1))
                mm.then_inc(s_down, 1)

            pe.wait_ge(s_w, 64)
            turn(0, 0, 0)
            up(0, 0)
            turn(1, 1, 0)

            def body(s, n, i):
                up(s, n)
                hidden_turn(s - 1, n - 1)
                turn(s + 1, n + 1, i)
                e = pe.value_load(slot_expert[0:1, bass.ds(s - 1, 1)], min_val=0, max_val=E - 1)
                down(s - 1, n - 1, e)

            for s in range(1, AHEAD):
                body(s, s, 0)
            with pe.Fori(0, (SLOTS - AHEAD) // RING) as i:
                for j in range(RING):
                    body(i * RING + (AHEAD + j), AHEAD + j, i)
            s = SLOTS - 1
            hidden_turn(s, s)
            down(s, s, pe.value_load(slot_expert[0:1, s:s + 1], min_val=0, max_val=E - 1))

            pe.wait_ge(s_xt, SLOTS + 1)
            for b in range(B):
                pe.wait_ge(s_add, KT * (b + 1))
                for j in range(2):
                    if b:
                        pe.wait_ge(s_oc, 2 * b + j - 1)
                    for q in range(4):
                        mm = pe.transpose(ps_x[j][:, q * P:(q + 1) * P], t_all[:, b * KT + 4 * j + q, :], ident[:, :])
                    mm.then_inc(s_ot, 1)

        @block.scalar
        def _(act):
            def copy_xt(s, n):
                act.wait_ge(s_turn, s + 1)
                if n >= 2:
                    act.wait_ge(s_up, s - 1)
                act.activation(xt[:, n % 2, :], ps_x[n % 2][:, 0:P], ACT.Copy).then_inc(s_xt, 1)

            def gelu(s, n):
                act.wait_ge(s_bias, s + 1)
                if n >= 2:
                    act.wait_ge(s_ht, s - 1)
                act.activation(hid[:, n % 2, :], hid_b[:, n % 2, :], ACT.Gelu).then_inc(s_gelu, 1)

            copy_xt(0, 0)
            copy_xt(1, 1)
            gelu(0, 0)

            def body(s, n):
                gelu(s, n)
                copy_xt(s + 1, n + 1)

            for s in range(1, AHEAD):
                body(s, s)
            with act.Fori(0, (SLOTS - AHEAD) // RING) as i:
                for j in range(RING):
                    body(i * RING + (AHEAD + j), AHEAD + j)

            for b in range(B):
                for j in range(2):
                    act.wait_ge(s_ot, 2 * b + j + 1)
                    if b:
                        act.wait_ge(s_out[j], 16 * b)
                    act.activation(out_t[:, j, :], ps_x[j][:, :], ACT.Copy).then_inc(s_oc, 1)

        @block.vector
        def _(dve):
            def bias(s, n):
                e = dve.value_load(slot_expert[0:1, bass.ds(s, 1)], min_val=0, max_val=E - 1)
                dve.wait_ge(s_up, s + 1)
                if n >= 2:
                    dve.wait_ge(s_gelu, s - 1)
                dve.tensor_tensor(hid_b[:, n % 2, :], ps_h[n % 2][:, :], tile_of(b1_sb, e), ALU.add).then_inc(s_bias, 1)

            def copy_ht(s, n):
                dve.wait_ge(s_ht, s + 1)
                if n >= 2:
                    dve.wait_ge(s_down, s - 1)
                dve.tensor_copy(hid_t[:, n % 2, :], ps_t[n % 2][:, :]).then_inc(s_htc, 1)

            def result(s, n, i):
                e = dve.value_load(slot_expert[0:1, bass.ds(s, 1)], min_val=0, max_val=E - 1)
                dve.wait_ge(s_down, s + 1)
                if n >= RING:
                    dve.wait_ge(s_st[n % RING], rounds(i, n) * 16)
                dve.tensor_tensor(y[:, n % RING, :], ps_y[n % 2][:, 0:C], tile_of(b2_sb, e), ALU.add).then_inc(s_y, 1)

            dve.wait_ge(s_w, 64)
            bias(0, 0)

            def body(s, n, i):
                bias(s, n)
                copy_ht(s - 1, n - 1)
                result(s - 1, n - 1, i)

            for s in range(1, AHEAD):
                body(s, s, 0)
            with dve.Fori(0, (SLOTS - AHEAD) // RING) as i:
                for j in range(RING):
                    body(i * RING + (AHEAD + j), AHEAD + j, i)
            s = SLOTS - 1
            copy_ht(s, s)
            result(s, s, 0)

            for t in range(TILES):
                dve.wait_ge(s_back[t // KT], 16 * KT)
                dve.scalar_tensor_tensor(out=t_all[:, t, :], in0=z_all[:, t, :], scalar=gain[:, t:t + 1],
                                         in1=t_all[:, t, :], op0=ALU.mult, op1=ALU.add).then_inc(s_add, 1)


def build(nc, x, w_proj, b_proj, w_out, b_out, wq, wk, wv, wr, br, w1, b1, w2, b2, out):
    rows_in = nc.dram_tensor("rows_in", [(SLOTS + 1) * P, C], F32).ap()
    rows_out = nc.dram_tensor("rows_out", [SLOTS * P, C], F32).ap()
    parts_dram = nc.dram_tensor("parts_dram", [2, 3, P, N], BF16).ap()

    def allocators(ctx):
        return (lambda n, s, d: ctx.enter_context(nc.sbuf_tensor(n, s, d)),
                lambda n, s, d: ctx.enter_context(nc.psum_tensor(n, s, d)),
                lambda n: ctx.enter_context(nc.semaphore(n)))

    with ExitStack() as top:
        sb, _, _ = allocators(top)
        t_all = sb("t_all", [P, TILES, C], F32)
        ident = sb("ident", [P, P], F32)
        identb = sb("identb", [P, P], BF16)
        with ExitStack() as ctx:
            attention_kernel(nc, *allocators(ctx), x, w_proj, b_proj, w_out, b_out, t_all, ident, identb, parts_dram)
        with ExitStack() as ctx:
            sb2, psum2, sem2 = allocators(ctx)
            mv, rstd = token_statistics(nc, sb2, sem2, t_all, "a")
            spike_kernel(nc, sb2, psum2, sem2, wq, wk, wv, t_all, mv, rstd, ident, rows_in)
        with ExitStack() as ctx:
            sb3, _, _ = allocators(ctx)
            z_all = sb3("z_all", [P, TILES, C], F32)
            pos = sb3("pos", [P, TILES], U32)
            slot_expert = sb3("slot_expert", [P, SLOTS], I32)
            gain = sb3("gain", [P, TILES], F32)
            with ExitStack() as ctx2:
                sb4, psum4, sem4 = allocators(ctx2)
                mv, rstd = token_statistics(nc, sb4, sem4, t_all, "b")
                routing_kernel(nc, sb4, psum4, sem4, wr, br, t_all, z_all, mv, rstd, ident, pos, slot_expert, gain)
            with ExitStack() as ctx2:
                expert_kernel(nc, *allocators(ctx2), w1, b1, w2, b2, z_all, t_all, ident, pos, slot_expert, gain,
                              rows_in, rows_out, out)


_INS = ['x', 'L0_conv_w_proj', 'L0_conv_b_proj', 'L0_conv_w_out', 'L0_conv_b_out', 'L1_attn_Wq', 'L1_attn_Wk',
        'L1_attn_Wv', 'L1_ffn_Wr', 'L1_ffn_br', 'L1_ffn_W1', 'L1_ffn_b1', 'L1_ffn_W2', 'L1_ffn_b2']


def kernel(**inputs):
    import numpy as _np
    import concourse.bacc as _bacc
    from concourse.bass_utils import run_bass_kernel_spmd as _run

    nc = _bacc.Bacc("TRN2", target_bir_lowering=False, num_devices=1)
    arrays, args = {}, []
    for name in _INS:
        a = _np.ascontiguousarray(inputs[name])
        if name == 'x':
            a = a.reshape(B, C, N)
        arrays[f"in_{name}"] = a
        args.append(nc.dram_tensor(f"in_{name}", a.shape, mybir.dt.from_np(a.dtype), kind="ExternalInput").ap())
    args.append(nc.dram_tensor("out_0", (B, C, N), F32, kind="ExternalOutput").ap())
    build(nc, *args)
    r = _run(nc, [arrays], core_ids=[0])
    return r.results[0]["out_0"].reshape(B, C, 32, 32)
```

```python
import concourse.bass as bass
from concourse import mybir
from contextlib import ExitStack

F32 = mybir.dt.float32
BF16 = mybir.dt.bfloat16
I32 = mybir.dt.int32
U32 = mybir.dt.uint32
ALU = mybir.AluOpType
ACT = mybir.ActivationFunctionType
AX = mybir.AxisListType

B, C, N = 8, 128, 1024
HEADS, DH = 8, 16
G = 2
HG = HEADS // G
P = 128
KT = N // P
HALF = N // 2
TILES = B * KT
QK_SCALE = DH ** -0.5
Q_THRESH, K_THRESH, V_THRESH, MASK_THRESH = 0.25, 0.25, 0.3, 0.1
LN_EPS = 1e-5
E, HID = 8, 512
SLOTS = TILES + E - 1

TERMS = [(0, 0), (0, 1), (1, 0), (1, 1), (0, 2), (2, 0)]
KROWS = DH * len(TERMS)
MROWS = 2
STACK_DMAS = 2 * len(TERMS)


BANKS_A = 6
ITEMS = KT * 2 * HG
RING_KINDS = ("score", "v", "proj", "max", "mrow", "sums", "spread", "out")


def max_jobs():
    jobs = []
    for h in range(HG):
        for qt in range(KT):
            for half in range(2):
                jobs.append(("max", (h, qt, half)))
            if h and qt == 2:
                jobs += [("mrow", (h - 1, 0)), ("mrow", (h - 1, 1))]
    return jobs


LAST_ROW = [("mrow", (HG - 1, 0)), ("mrow", (HG - 1, 1))]


def finish_jobs(g):
    jobs = [(8, "sums", ()), (15, "spread", (0,)), (15, "spread", (1,))]
    if g == 1:
        jobs += [(19 + j, "out", (j,)) for j in range(4)]
    return jobs


def step_list(g, first=False, project=True, ahead=True):
    nxt = 1 - g
    side = []
    if not first:
        side += [(2, "pv", (nxt, 15))] + finish_jobs(nxt)
    if ahead:
        side.append((3, "v", (nxt,)))
        if g == 0 and project:
            side += [(11 + n, "proj", (n // 2, n % 2)) for n in range(4)]
        jobs = max_jobs()
        side += [(12 + n * 43 // len(jobs),) + job for n, job in enumerate(jobs)]
        side += [(59,) + job for job in LAST_ROW]
    side.sort(key=lambda j: j[0])
    out = []
    for i in range(ITEMS):
        out.append((g, "score", (i,)))
        if i >= 6 and i % 4 == 2:
            out.append((g, "pv", (g, (i - 6) // 4)))
        while side and side[0][0] <= i:
            out.append((g,) + side.pop(0)[1:])
    return out


def first_list():
    jobs = [("proj", (n // 2, n % 2)) for n in range(4)] + [("v", (0,))] + max_jobs() + LAST_ROW
    return [(1,) + job for job in jobs] + step_list(0, first=True)


def last_list():
    jobs = [("pv", (1, 15))] + [job[1:] for job in finish_jobs(1)]
    return step_list(1, ahead=False) + [(0,) + job for job in jobs]


START = first_list()
BODY = step_list(1) + step_list(0)
BEFORE_LAST = step_list(1) + step_list(0, project=False)
END = last_list()


def ring_uses(jobs):
    return sum(kind in RING_KINDS for _, kind, _ in jobs)


def use_of(jobs, g, kind, args):
    return ring_uses(jobs[:jobs.index((g, kind, args))])


LOOPS = B - 2
R0, RB = ring_uses(START), ring_uses(BODY)
R_END = R0 + LOOPS * RB + ring_uses(BEFORE_LAST)
assert RB % BANKS_A == 0


def step_start(base, jobs, g):
    return base + ring_uses(jobs[:[job[0] for job in jobs].index(g)])


def filled(b, n):
    return b * RB + (n + 1)


def emptied(b, n):
    return n % BANKS_A, b * (RB // BANKS_A) + (n // BANKS_A + 1)


def wait_emptied(eng, s_empty, b, uses):
    latest = {}
    for n in uses:
        if n >= 0:
            latest[n % BANKS_A] = max(n, latest.get(n % BANKS_A, -1))
    for n in latest.values():
        bank, count = emptied(b, n)
        eng.wait_ge(s_empty[bank], count)


def attention_kernel(nc, sb, psum, sem, x, w_proj, b_proj, w_out, b_out, t_all, ident, identb, parts_dram):
    xp = sb("xp", [P, N], F32)
    xr = sb("xr", [P, N], F32)
    w_qk = [sb(f"w_qk{s}", [C, P], F32) for s in range(2)]
    b_qk = [sb(f"b_qk{s}", [P, 1], F32) for s in range(2)]
    b_q = sb("b_q", [P, 1], F32)
    w_v = [sb(f"w_v{g}", [C, HG * DH], F32) for g in range(G)]
    b_v = [sb(f"b_v{g}", [P, HG * DH], F32) for g in range(G)]
    w_o = sb("w_o", [P, G, C], F32)
    b_o = sb("b_o", [P, C], F32)
    pick = sb("pick", [P, HG], F32)
    full = [[sb(f"full{s}{h}", [P, HALF], F32) for h in range(2)] for s in range(2)]
    rest = sb("rest", [P, HALF], F32)
    parts = [[sb(f"part{s}{c}", [P, N], BF16) for c in range(3)] for s in range(2)]
    stack = [[sb(f"stack{s}{g}", [P, HG, N], BF16) for g in range(G)] for s in range(2)]
    v_sb = [sb(f"v_sb{g}", [P, KT, HG, 32], F32) for g in range(G)]
    probs = sb("probs", [P, 2, HG, N], F32)
    mx = sb("mx", [P, HG, KT, 2], F32)
    m_all = sb("m_all", [P, KT], F32)
    m_parts = sb("m_parts", [P, HG, KT, MROWS], BF16)
    o_sb = sb("o_sb", [P, 2, HALF], F32)
    inv = sb("inv", [P, KT, HG], F32)
    o_n = [sb(f"o_n{g}", [P, N], F32) for g in range(G)]

    ring = [psum(f"ring{i}", [P, HALF], F32) for i in range(BANKS_A)]
    outT = [psum(f"outT{i}", [P, HALF], F32) for i in range(2)]

    s_w = sem("s_w")
    s_xp = sem("s_xp")
    s_xr = sem("s_xr")
    s_const = sem("s_const")
    s_bq = sem("s_bq")
    s_fill = sem("s_fill")
    s_empty = [sem(f"s_empty{i}") for i in range(BANKS_A)]
    s_split = sem("s_split")
    s_parts = sem("s_parts")
    s_gp = sem("s_gp")
    s_passed = sem("s_passed")
    s_stack = [sem(f"s_stack{g}") for g in range(G)]
    s_mcol = sem("s_mcol")
    s_mm = sem("s_mm")
    s_pv = sem("s_pv")
    s_osb = sem("s_osb")

    def w_part(part):
        return w_proj.rearrange("c (h t) -> c h t", t=3 * DH)[:, :, part * DH:(part + 1) * DH]

    N_CONST = 1 + 2 * G + 3
    SUM_ROW = DH

    with nc.Block() as block:
        @block.sync
        def _(sp):
            sp.dma_start(xp[:, :], x[0]).then_inc(s_xp, 16)
            for s in range(2):
                sp.dma_start(w_qk[s][:, :].rearrange("c (h d) -> c h d", d=DH), w_part(s)).then_inc(s_w, 16)
                sp.dma_start(b_qk[s][:, :],
                             b_proj.rearrange("(h t d) -> t h d", h=HEADS, t=3)[s].unsqueeze(2)).then_inc(s_w, 16)
            for g in range(G):
                heads = slice(g * HG, (g + 1) * HG)
                sp.dma_start(w_v[g][:, :].rearrange("c (h d) -> c h d", d=DH), w_part(2)[:, heads, :]).then_inc(s_w, 16)
                sp.dma_start(b_v[g][:, :].rearrange("p (h d) -> p h d", d=DH),
                             b_proj.rearrange("(h t d) -> t h d", h=HEADS, t=3)[2, heads].partition_broadcast(P)
                             ).then_inc(s_w, 16)
            sp.dma_start(b_o[:, :], b_out.partition_broadcast(P)).then_inc(s_w, 16)
            sp.wait_ge(s_const, 1)
            for g in range(G):
                for h in range(HG):
                    r = (g * HG + h) * DH
                    sp.dma_start(w_o[32 * h:32 * h + DH, g, :], w_out[r:r + DH, :]).then_inc(s_w, 16)
            sp.dma_start(xr[:, :], x[0]).then_inc(s_xr, 16)

            def put_parts():
                for s in range(2):
                    for c in range(3):
                        sp.dma_start(parts_dram[s, c], parts[s][c][:, :]).then_inc(s_parts, 16)

            def stack_up(g):
                for n, pair in enumerate(TERMS):
                    for s in range(2):
                        src = parts_dram[s, pair[s], g * HG * DH:(g + 1) * HG * DH, :]
                        sp.dma_start(stack[s][g][n * DH:(n + 1) * DH, :, :],
                                     src.rearrange("(h d) n -> d h n", d=DH)).then_inc(s_stack[g], 16)

            sp.wait_ge(s_split, 4)
            put_parts()
            sp.wait_ge(s_parts, 96)
            for g in range(G):
                stack_up(g)
            sp.wait_ge(s_fill, filled(0, use_of(START, 0, "v", (1,))))
            sp.dma_start(xp[:, :], x[1]).then_inc(s_xp, 16)
            sp.wait_ge(s_split, 8)
            put_parts()

            def batch(b, jobs, more):
                sp.wait_ge(s_fill, b * RB + R0)
                sp.wait_ge(s_parts, b * 96 + 192)
                stack_up(0)
                sp.wait_ge(s_fill, filled(b, R0 + use_of(jobs, 1, "score", (ITEMS - 1,))))
                stack_up(1)
                if more:
                    sp.wait_ge(s_fill, filled(b, R0 + use_of(jobs, 0, "v", (1,))))
                    sp.dma_start(xp[:, :], x[b + 2]).then_inc(s_xp, 16)
                sp.wait_ge(s_fill, filled(b, R0 + use_of(jobs, 0, "out", (3,))))
                sp.dma_start(xr[:, :], x[b + 1]).then_inc(s_xr, 16)
                if more:
                    sp.wait_ge(s_split, b * 4 + 12)
                    put_parts()

            with sp.Fori(0, LOOPS) as b:
                batch(b, BODY, True)
            batch(LOOPS, BEFORE_LAST, False)

        @block.gpsimd
        def _(pool):
            pool.memset(w_o[:, :, :], 0.0).then_inc(s_const, 1)
            pool.memset(pick[:, :], 0.0).then_inc(s_gp, 1)
            pool.memset(ident[:, :], 0.0).then_inc(s_gp, 1)
            pool.memset(identb[:, :], 0.0).then_inc(s_gp, 1)
            for g in range(G):
                pool.memset(v_sb[g][:, :, :, DH:32], 1.0).then_inc(s_const, 1)
                pool.wait_ge(s_const, 2 * g + 2)
                pool.memset(stack[1][g][KROWS:KROWS + MROWS, :, :], 1.0).then_inc(s_const, 1)
                pool.wait_ge(s_const, 2 * g + 3)
            pool.wait_ge(s_gp, 3)
            pool.affine_select(out=pick[:, :], in_=pick[:, :], compare_op=ALU.not_equal, fill=1.0, base=-SUM_ROW,
                               pattern=[[-32, HG]], channel_multiplier=1).then_inc(s_const, 1)
            for m in (ident, identb):
                pool.affine_select(out=m[:, :], in_=m[:, :], compare_op=ALU.not_equal, fill=1.0, base=0,
                                   pattern=[[-1, P]], channel_multiplier=1).then_inc(s_const, 1)

            def settled():
                pool.sem_inc(s_passed, 1)

            def split(b, batch, base, jobs, g):
                chain, first = batch * 16 + 3, batch * 4
                for n in range(4):
                    s, half = n // 2, n % 2
                    cols = slice(half * HALF, (half + 1) * HALF)
                    src, part = full[s][half], parts[s]
                    wait_emptied(pool, s_empty, b, [base + use_of(jobs, g, "proj", (s, half))])
                    settled()
                    pool.tensor_copy(part[0][:, cols], src[:, :]).then_inc(s_gp, 1)
                    pool.wait_ge(s_gp, chain + (4 * n + 1))
                    pool.tensor_tensor(rest[:, :], src[:, :], part[0][:, cols], ALU.subtract).then_inc(s_gp, 1)
                    pool.wait_ge(s_gp, chain + (4 * n + 2))
                    settled()
                    pool.tensor_copy(part[1][:, cols], rest[:, :]).then_inc(s_gp, 1)
                    pool.wait_ge(s_gp, chain + (4 * n + 3))
                    pool.tensor_tensor(part[2][:, cols], rest[:, :], part[1][:, cols], ALU.subtract).then_inc(s_split, 1)
                    pool.wait_ge(s_split, first + (n + 1))
                    pool.sem_inc(s_gp, 1)

            def parts_free(batch):
                pool.wait_ge(s_parts, batch * 96)
                for g in range(G):
                    pool.wait_ge(s_stack[g], batch * (16 * STACK_DMAS))

            split(0, 0, 0, START, 1)
            parts_free(1)
            split(0, 1, 0, START, 0)
            with pool.Fori(0, LOOPS) as b:
                parts_free(b + 2)
                split(b, b + 2, R0, BODY, 0)

        @block.tensor
        def _(pe):
            def run(b, base, jobs, batch_of, step_of):
                n = base
                rows = [base - 6, base - 5] if base else []
                for g, kind, args in jobs:
                    nxt = 1 - g
                    if kind == "pv":
                        gg, j = args
                        kt, half = j // 2, j % 2
                        step = step_of[g] if gg == g else step_of[g] - 1
                        done = base + use_of(jobs, g, "score", (4 * j + 3,)) if gg == g else \
                            step_start(base, jobs, g) - 1
                        wait_emptied(pe, s_empty, b, [done])
                        if kt == 0 and not (isinstance(step, int) and step == 0):
                            pe.wait_ge(s_osb, step * 2 + (half - 1))
                        for h in range(HG):
                            mm = pe.matmul(outT[half][32 * h:32 * h + 32, :], v_sb[gg][:, kt, h, :],
                                           probs[:, kt % 2, h, half * HALF:(half + 1) * HALF],
                                           start=(kt == 0), stop=(kt == KT - 1))
                        mm.then_inc(s_pv, 1)
                        continue
                    needs = [n - BANKS_A]
                    if kind == "mrow":
                        rows = rows[-1:] + [n]
                    if kind == "score" and args[0] == 0:
                        needs += rows
                    if kind == "spread":
                        needs.append(base + use_of(jobs, g, "sums", ()))
                    if kind == "out":
                        needs.append(base + use_of(jobs, g, "spread", (args[0] // 2,)))
                    wait_emptied(pe, s_empty, b, needs)
                    out = ring[n % BANKS_A]
                    if kind == "score":
                        kt, half, h = args[0] // 8, args[0] // 4 % 2, args[0] % 4
                        mm = pe.matmul(out[:, :], stack[1][g][0:KROWS + MROWS, h, kt * P:(kt + 1) * P],
                                       stack[0][g][0:KROWS + MROWS, h, half * HALF:(half + 1) * HALF],
                                       start=True, stop=True)
                    elif kind == "proj":
                        s, half = args
                        if s == 0 and half == 0 and g == 0:
                            pe.wait_ge(s_xp, batch_of[0] * 16 + 32)
                        mm = pe.matmul(out[:, :], w_qk[s][:, :], xp[:, half * HALF:(half + 1) * HALF],
                                       start=True, stop=True)
                    elif kind == "v":
                        for kt in range(KT):
                            mm = pe.matmul(out[:, kt * 64:(kt + 1) * 64], xp[:, kt * P:(kt + 1) * P],
                                           w_v[args[0]][:, :], start=True, stop=True)
                    elif kind == "max":
                        h, qt, half = args
                        if args == (0, 0, 0):
                            pe.wait_ge(s_stack[nxt], stacks_of(g, batch_of) * (16 * STACK_DMAS))
                        mm = pe.matmul(out[:, :], stack[0][nxt][0:KROWS, h, qt * P:(qt + 1) * P],
                                       stack[1][nxt][0:KROWS, h, half * HALF:(half + 1) * HALF], start=True, stop=True)
                    elif kind == "mrow":
                        h, half = args
                        if half == 0:
                            pe.wait_ge(s_mm, step_of[g] * HG + (HG + h + 1))
                        for q in range(KT // 2):
                            mm = pe.matmul(out[KROWS:KROWS + MROWS, q * P:(q + 1) * P],
                                           m_parts[:, h, half * (KT // 2) + q, :], identb[:, :], start=True, stop=True)
                    elif kind == "sums":
                        pe.wait_ge(s_osb, step_of[g] * 2)
                        for q in range(KT):
                            mm = pe.matmul(out[:, q * HG:(q + 1) * HG],
                                           o_sb[:, q // 4, q % 4 * P:(q % 4 + 1) * P], pick[:, :], start=True, stop=True)
                    elif kind == "spread":
                        for q in range(KT // 2):
                            for h in range(HG):
                                mm = pe.matmul(out[32 * h:32 * h + 32, q * P:(q + 1) * P],
                                               inv[:, args[0] * 4 + q, h:h + 1].broadcast_to([P, 32]),
                                               ident[:, :], start=True, stop=True)
                    elif kind == "out":
                        if args[0] == 0:
                            pe.wait_ge(s_xr, batch_of[1] * 16 + 16)
                        for q in range(2):
                            tok = slice((args[0] * 2 + q) * P, (args[0] * 2 + q + 1) * P)
                            dst = out[:, q * C:(q + 1) * C]
                            pe.matmul(dst, o_n[0][:, tok], w_o[:, 0, :], start=True, stop=False)
                            pe.matmul(dst, o_n[1][:, tok], w_o[:, 1, :], start=False, stop=False)
                            mm = pe.matmul(dst, xr[:, tok], ident[:, :], start=False, stop=True)
                    mm.then_inc(s_fill, 1)
                    n += 1

            def stacks_of(g, batch_of):
                return batch_of[g] + (1 if g == 0 else 2)

            pe.sem_inc(s_pv, 4)
            pe.wait_ge(s_w, 16 * (4 + 2 * G + 1 + HEADS))
            pe.wait_ge(s_xp, 16)
            pe.wait_ge(s_const, N_CONST)
            run(0, 0, START, {0: 0, 1: -1}, {0: 0, 1: -1})
            with pe.Fori(0, LOOPS) as b:
                run(b, R0, BODY, {1: b, 0: b + 1}, {1: b * 2 + 1, 0: b * 2 + 2})
            run(LOOPS, R0, BEFORE_LAST, {1: LOOPS, 0: LOOPS + 1}, {1: LOOPS * 2 + 1, 0: LOOPS * 2 + 2})
            run(0, R_END, END, {1: B - 1, 0: B}, {1: 2 * B - 1, 0: 2 * B})

        @block.scalar
        def _(act):
            def copy_out(step, half):
                act.wait_ge(s_pv, step * 16 + (3 + half))
                act.activation(o_sb[:, half, :], outT[half][:, :], ACT.Copy).then_inc(s_osb, 1)

            def run(b, base, jobs, batch_of, step_of):
                n = base - 1
                for g, kind, args in jobs:
                    if kind not in RING_KINDS:
                        continue
                    n += 1
                    if kind not in ("score", "mrow", "proj"):
                        continue
                    bank, _ = emptied(b, n)
                    if kind == "score" and args[0] % 4 == 0:
                        act.wait_ge(s_pv, step_of[g] * 16 + (args[0] // 4 + 1))
                    if kind == "proj" and not (g == 1):
                        act.wait_ge(s_split, batch_of[0] * 4 + 4)
                    act.wait_ge(s_fill, filled(b, n))
                    ps = ring[bank]
                    if kind == "score":
                        kt, half, h = args[0] // 8, args[0] // 4 % 2, args[0] % 4
                        act.activation(probs[:, kt % 2, h, half * HALF:(half + 1) * HALF], ps[:, :],
                                       ACT.Exp).then_inc(s_empty[bank], 1)
                        if args[0] in (1, 4) and not (isinstance(step_of[g], int) and step_of[g] == 0):
                            copy_out(step_of[g], args[0] // 4)
                    elif kind == "mrow":
                        h, half = args
                        act.activation(stack[0][1 - g][KROWS:KROWS + MROWS, h, half * HALF:(half + 1) * HALF],
                                       ps[KROWS:KROWS + MROWS, :], ACT.Copy).then_inc(s_empty[bank], 1)
                    elif kind == "proj":
                        s, half = args
                        act.activation(full[s][half][:, :], ps[:, :], ACT.Identity,
                                       bias=(b_q if s == 0 else b_qk[1])[:, 0:1],
                                       scale=QK_SCALE if s == 0 else 1.0).then_inc(s_empty[bank], 1)

            act.wait_ge(s_bq, 1)
            run(0, 0, START, {0: 0, 1: -1}, {0: 0, 1: -1})
            with act.Fori(0, LOOPS) as b:
                run(b, R0, BODY, {1: b, 0: b + 1}, {1: b * 2 + 1, 0: b * 2 + 2})
            run(LOOPS, R0, BEFORE_LAST, {1: LOOPS, 0: LOOPS + 1}, {1: LOOPS * 2 + 1, 0: LOOPS * 2 + 2})
            run(0, R_END, END, {1: B - 1, 0: B}, {1: 2 * B - 1, 0: 2 * B})
            for half in range(2):
                copy_out(2 * B, half)

        @block.vector
        def _(dve):
            def run(b, base, jobs, batch_of, step_of):
                n, before = base - 1, None
                for g, kind, args in jobs:
                    if kind not in RING_KINDS:
                        continue
                    n += 1
                    if kind not in ("v", "max", "sums", "spread", "out"):
                        continue
                    bank, _ = emptied(b, n)
                    dve.wait_ge(s_fill, filled(b, n))
                    ps = ring[bank]
                    if kind == "v":
                        gg = args[0]
                        dve.tensor_tensor(v_sb[gg][:, :, :, 0:DH],
                                          ps[:, :].rearrange("p (k h d) -> p k h d", k=KT, d=DH),
                                          b_v[gg][:, :].rearrange("p (h d) -> p h d", d=DH).unsqueeze(1)
                                          .broadcast_to([P, KT, HG, DH]), ALU.add).then_inc(s_empty[bank], 1)
                    elif kind == "max":
                        h, qt, half = args
                        dve.tensor_reduce(mx[:, h, qt, half:half + 1], ps[:, :], AX.X,
                                          ALU.max).then_inc(s_empty[bank], 1)
                        if qt == KT - 1 and half == 1:
                            done = step_of[g] * HG + (HG + h)
                            wait_emptied(dve, s_empty, b, [before, n])
                            dve.tensor_reduce(m_all[:, :], mx[:, h, :, :], AX.X, ALU.max).then_inc(s_mcol, 1)
                            dve.wait_ge(s_mcol, done * 2 + 1)
                            dve.tensor_scalar(m_parts[:, h, :, 0], m_all[:, :], -1.0, None,
                                              ALU.mult).then_inc(s_mcol, 1)
                            dve.wait_ge(s_mcol, done * 2 + 2)
                            dve.scalar_tensor_tensor(out=m_parts[:, h, :, 1], in0=m_all[:, :], scalar=-1.0,
                                                     in1=m_parts[:, h, :, 0], op0=ALU.mult,
                                                     op1=ALU.subtract).then_inc(s_mm, 1)
                            dve.wait_ge(s_mm, done + 1)
                        before = n
                    elif kind == "sums":
                        dve.reciprocal(inv[:, :, :], ps[:, 0:KT * HG].rearrange("p (k h) -> p k h", h=HG)
                                       ).then_inc(s_empty[bank], 1)
                    elif kind == "spread":
                        half = args[0]
                        dve.tensor_tensor(o_n[1 - g][:, half * HALF:(half + 1) * HALF], o_sb[:, half, :], ps[:, :],
                                          ALU.mult).then_inc(s_empty[bank], 1)
                    elif kind == "out":
                        first = batch_of[1] * KT + args[0] * 2
                        dve.tensor_tensor(t_all[:, bass.ds(first, 2), :],
                                          ps[:, 0:2 * C].rearrange("p (q c) -> p q c", c=C),
                                          b_o[:, :].unsqueeze(1).broadcast_to([P, 2, C]),
                                          ALU.add).then_inc(s_empty[bank], 1)

            dve.wait_ge(s_w, 16 * (4 + 2 * G + 1 + HEADS))
            dve.wait_ge(s_const, N_CONST)
            dve.tensor_scalar(b_q[:, :], b_qk[0][:, :], QK_SCALE, None, ALU.mult).then_inc(s_bq, 1)
            run(0, 0, START, {0: 0, 1: -1}, {0: 0, 1: -1})
            with dve.Fori(0, LOOPS) as b:
                run(b, R0, BODY, {1: b, 0: b + 1}, {1: b * 2 + 1, 0: b * 2 + 2})
            run(LOOPS, R0, BEFORE_LAST, {1: LOOPS, 0: LOOPS + 1}, {1: LOOPS * 2 + 1, 0: LOOPS * 2 + 2})
            run(0, R_END, END, {1: B - 1, 0: B}, {1: 2 * B - 1, 0: 2 * B})


def tile_of(ap, n):
    return ap[:, bass.ds(n, 1), :].rearrange("p a s -> p (a s)")


def token_statistics(nc, sb, sem, t_all, tag):
    stats = sb(f"stats{tag}", [P, TILES, 6], F32)
    mv = sb(f"mv{tag}", [P, TILES, 2], F32)
    std = sb(f"std{tag}", [P, TILES], F32)
    rstd = sb(f"rstd{tag}", [P, TILES], F32)
    s_stat = sem(f"s_stat{tag}")
    s_std = sem(f"s_std{tag}")
    with nc.Block() as block:
        @block.vector
        def _(dve):
            with dve.Fori(0, B) as b:
                for k in range(KT):
                    dve.bn_stats(tile_of(stats, b * KT + k), tile_of(t_all, b * KT + k)).then_inc(s_stat, 1)
            dve.wait_ge(s_stat, TILES)
            for k in range(TILES):
                last = dve.bn_aggr(mv[:, k, :], stats[:, k, :])
            last.then_inc(s_stat, 1)
            dve.wait_ge(s_stat, TILES + 1)
            dve.tensor_scalar(std[:, :], mv[:, :, 1], LN_EPS, None, ALU.add).then_inc(s_stat, 1)
            dve.wait_ge(s_std, 1)
            dve.reciprocal(rstd[:, :], std[:, :])

        @block.scalar
        def _(act):
            act.wait_ge(s_stat, TILES + 2)
            act.activation(std[:, :], std[:, :], ACT.Sqrt).then_inc(s_std, 1)
    return mv, rstd


def normalise(eng, out, t_all, mv, rstd, n):
    return eng.tensor_scalar(out, tile_of(t_all, n), mv[:, bass.ds(n, 1), 0], rstd[:, bass.ds(n, 1)],
                             ALU.subtract, ALU.mult)


BANKS = 8
MASKS = [(m, lo, min(lo + HALF, N)) for m in range(KT) for lo in range(m * P, N, HALF)]
TURN_SPIKE = [("turn", (j,)) for j in range(2)] + [("spike", (s, half)) for s in range(2) for half in range(2)]
SPIKE_V = [("spike_v", (j,)) for j in range(2)]
COUNT = [("count", (j,)) for j in range(4)]
MASK = [("mask", m) for m in MASKS]
SPIKE_FIRST = TURN_SPIKE + SPIKE_V
SPIKE_BODY = MASK + TURN_SPIKE + COUNT + SPIKE_V
SPIKE_LAST = MASK + COUNT
assert len(SPIKE_FIRST) == BANKS and len(SPIKE_BODY) % BANKS == 0


def spike_use(b, n):
    return n % BANKS, b * (len(SPIKE_BODY) // BANKS) + (BANKS + n) // BANKS


def spike_kernel(nc, sb, psum, sem, wq, wk, wv, t_all, mv, rstd, ident, rows_in):
    w_raw = sb("w_raw", [P, 3, C], F32)
    w_t = sb("w_t", [P, 3, C], F32)
    zeros = sb("zeros", [P, C], F32)
    z = sb("z", [P, KT, C], F32)
    zt = sb("zt", [P, N], F32)
    spikes = [sb(f"spikes{s}", [P, N], BF16) for s in range(2)]
    spikes_v = sb("spikes_v", [P, KT, C], BF16)
    mask = sb("mask", [P, KT, N], BF16)
    causal = sb("causal", [P, P], BF16)
    bank = [psum(f"bank{i}", [P, HALF], F32) for i in range(BANKS)]
    s_w = sem("sp_w")
    s_c = sem("sp_c")
    s_wt = sem("sp_wt")
    s_wc = sem("sp_wc")
    s_z = sem("sp_z")
    s_fill = sem("sp_fill")
    s_zero = sem("sp_zero")
    s_empty = [sem(f"sp_empty{i}") for i in range(BANKS)]

    with nc.Block() as block:
        @block.sync
        def _(sp):
            for n, w in enumerate((wq, wk, wv)):
                sp.dma_start(w_raw[:, n, :], w).then_inc(s_w, 16)
            sp.wait_ge(s_c, 3)
            sp.dma_start(rows_in.rearrange("(s p) c -> p s c", p=P),
                         zeros[:, :].unsqueeze(1).broadcast_to([P, SLOTS + 1, C])).then_inc(s_zero, 16)
            sp.wait_ge(s_zero, 16)

        @block.gpsimd
        def _(pool):
            pool.memset(causal[:, :], 1.0).then_inc(s_c, 1)
            pool.wait_ge(s_c, 1)
            pool.affine_select(out=causal[:, :], in_=causal[:, :], compare_op=ALU.is_ge, fill=0.0, base=0,
                               pattern=[[1, P]], channel_multiplier=-1).then_inc(s_c, 1)
            pool.memset(zeros[:, :], 0.0).then_inc(s_c, 1)

        @block.tensor
        def _(pe):
            pe.wait_ge(s_w, 48)
            for n in range(3):
                mm = pe.transpose(bank[0][:, n * C:(n + 1) * C], w_raw[:, n, :], ident[:, :])
            mm.then_inc(s_wt, 1)
            pe.wait_ge(s_wc, 1)

            def use(b, n, kind, args, tiles):
                i, emptied = spike_use(b, n)
                out = bank[i]
                if kind == "mask" and args[0] == 0 and args[1] == 0:
                    for back in range(1, BANKS + 1):
                        j, before = spike_use(b, n - back)
                        pe.wait_ge(s_empty[j], before + 1)
                elif kind == "count" and args[0] == 0:
                    for m in range(n - BANKS, len(MASKS)):
                        j, before = spike_use(b, m)
                        pe.wait_ge(s_empty[j], before + 1)
                elif b is not None and not (n < 0):
                    pe.wait_ge(s_empty[i], emptied)
                if kind == "turn":
                    pe.wait_ge(s_z, tiles)
                    for q in range(4):
                        mm = pe.transpose(out[:, q * P:(q + 1) * P], z[:, args[0] * 4 + q, :], ident[:, :])
                elif kind == "spike":
                    s, half = args
                    if s == 0:
                        j, before = spike_use(b, n - 2)
                        pe.wait_ge(s_empty[j], before + 1)
                    mm = pe.matmul(out[:, :], w_t[:, s, :], zt[:, half * HALF:(half + 1) * HALF], start=True, stop=True)
                elif kind == "spike_v":
                    for q in range(4):
                        tok = args[0] * 4 + q
                        mm = pe.matmul(out[:, q * C:(q + 1) * C], zt[:, tok * P:(tok + 1) * P], w_t[:, 2, :],
                                       start=True, stop=True)
                elif kind == "mask":
                    m, lo, hi = args
                    mm = pe.matmul(out[:, 0:hi - lo], spikes[1][:, m * P:(m + 1) * P], spikes[0][:, lo:hi],
                                   start=True, stop=True)
                elif kind == "count":
                    for q in range(2):
                        l = args[0] * 2 + q
                        for m in range(l + 1):
                            mm = pe.matmul(out[:, q * C:(q + 1) * C], mask[:, m, l * P:(l + 1) * P],
                                           spikes_v[:, m, :], start=(m == 0), stop=(m == l))
                mm.then_inc(s_fill, 1)

            for n, (kind, args) in enumerate(SPIKE_FIRST):
                use(0, n - BANKS, kind, args, KT)
            with pe.Fori(0, B - 1) as b:
                for n, (kind, args) in enumerate(SPIKE_BODY):
                    use(b, n, kind, args, b * KT + 2 * KT)
            for n, (kind, args) in enumerate(SPIKE_LAST):
                use(B - 1, n, kind, args, 0)

        @block.scalar
        def _(act):
            act.wait_ge(s_wt, 1)
            act.activation(w_t[:, :, :], bank[0][:, 0:3 * C].rearrange("p (n c) -> p n c", n=3),
                           ACT.Copy).then_inc(s_wc, 1)

            def turned(b, n, j):
                i, _ = spike_use(b, n)
                act.wait_ge(s_fill, b * len(SPIKE_BODY) + (BANKS + n + 1))
                act.activation(zt[:, j * HALF:(j + 1) * HALF], bank[i][:, :], ACT.Copy).then_inc(s_empty[i], 1)

            for j in range(2):
                turned(0, j - BANKS, j)
            with act.Fori(0, B - 1) as b:
                for j in range(2):
                    turned(b, len(MASKS) + j, j)

        @block.vector
        def _(dve):
            def normalise_batch(b):
                for k in range(KT):
                    normalise(dve, z[:, k, :], t_all, mv, rstd, b * KT + k).then_inc(s_z, 1)

            def use(b, n, kind, args):
                i, emptied = spike_use(b, n)
                if kind == "turn":
                    return
                dve.wait_ge(s_fill, b * len(SPIKE_BODY) + (BANKS + n + 1))
                ps = bank[i]
                if kind == "spike":
                    s, half = args
                    dve.tensor_scalar(spikes[s][:, half * HALF:(half + 1) * HALF], ps[:, :], (Q_THRESH, K_THRESH)[s],
                                      None, ALU.is_ge).then_inc(s_empty[i], 1)
                elif kind == "spike_v":
                    dve.tensor_scalar(spikes_v[:, args[0] * 4:args[0] * 4 + 4, :],
                                      ps[:, :].rearrange("p (q c) -> p q c", c=C), V_THRESH, None,
                                      ALU.is_ge).then_inc(s_empty[i], 1)
                elif kind == "mask":
                    m, lo, hi = args
                    at = lo
                    if lo == m * P:
                        last = dve.scalar_tensor_tensor(out=mask[:, m, lo:lo + P], in0=ps[:, 0:P], scalar=MASK_THRESH,
                                                        in1=causal[:, :], op0=ALU.is_gt, op1=ALU.mult)
                        at = lo + P
                    if at < hi:
                        last = dve.tensor_scalar(mask[:, m, at:hi], ps[:, at - lo:hi - lo], MASK_THRESH, None, ALU.is_gt)
                    last.then_inc(s_empty[i], 1)
                elif kind == "count":
                    tiles = t_all[:, bass.ds(b * KT + args[0] * 2, 2), :]
                    dve.tensor_tensor(tiles, tiles, ps[:, 0:2 * C].rearrange("p (q c) -> p q c", c=C),
                                      ALU.add).then_inc(s_empty[i], 1)

            dve.wait_ge(s_c, 3)
            normalise_batch(0)
            for n, (kind, args) in enumerate(SPIKE_FIRST):
                use(0, n - BANKS, kind, args)
            with dve.Fori(0, B - 1) as b:
                normalise_batch(b + 1)
                for n, (kind, args) in enumerate(SPIKE_BODY):
                    use(b, n, kind, args)
            for n, (kind, args) in enumerate(SPIKE_LAST):
                use(B - 1, n, kind, args)


def routing_kernel(nc, sb, psum, sem, wr, br, t_all, z_all, mv, rstd, ident, pos, slot_expert, gain):
    w_r = sb("w_r", [P, E], F32)
    b_r = sb("b_r", [P, E], F32)
    zt = sb("r_zt", [P, 2, HALF], F32)
    before = sb("before", [P, P], BF16)
    ones = sb("ones", [P, P], BF16)
    rank = sb("rank", [P, E], F32)
    slot_no = sb("slot_no", [P, SLOTS], F32)
    logit = sb("logit", [P, TILES, E], F32)
    prob = sb("prob", [P, TILES, E], F32)
    work = sb("work", [P, TILES, E], F32)
    chosen = sb("chosen", [P, TILES, E], BF16)
    col = [sb(f"col{i}", [P, TILES], F32) for i in range(6)]
    keep = sb("keep", [P, E, TILES], F32)
    count = sb("count", [P, E, TILES], F32)
    upto = sb("upto", [P, E, TILES], F32)
    total = sb("total", [P, E], F32)
    total_i = sb("total_i", [P, E], I32)
    tiles_i = sb("tiles_i", [P, E], I32)
    tiles_e = sb("tiles_e", [P, E], F32)
    end_e = sb("end_e", [P, E], F32)
    base_e = sb("base_e", [P, E], F32)
    ones_e = sb("ones_e", [P, E], F32)
    past = sb("past", [P, SLOTS, E], F32)
    slot_f = sb("slot_f", [P, SLOTS], F32)
    ps_t = [psum(f"r_turn{i}", [P, HALF], F32) for i in range(2)]
    ps_logit = psum("ps_logit", [P, TILES * E], F32)
    ps_before = psum("ps_before", [P, TILES * E], F32)
    ps_count = psum("ps_count", [P, TILES * E], F32)
    s_w = sem("r_w")
    s_c = sem("r_c")
    s_z = sem("r_z")
    s_turn = sem("r_turn")
    s_zt = sem("r_zt")
    s_logit = sem("r_logit")
    s_shift = sem("r_shift")
    s_exp = sem("r_exp")
    s_chosen = sem("r_chosen")
    s_sum = sem("r_sum")
    s_v = sem("r_v")
    DVE_CONST = 2

    with nc.Block() as block:
        @block.sync
        def _(sp):
            sp.dma_start(w_r[:, :], wr).then_inc(s_w, 16)
            sp.dma_start(b_r[:, :], br.partition_broadcast(P)).then_inc(s_w, 16)

        @block.gpsimd
        def _(pool):
            pool.memset(before[:, :], 1.0).then_inc(s_c, 1)
            pool.memset(ones[:, :], 1.0).then_inc(s_c, 1)
            pool.memset(ones_e[:, :], 1.0).then_inc(s_c, 1)
            pool.memset(keep[:, :, 1:TILES], 1.0).then_inc(s_c, 1)
            pool.memset(keep[:, :, 0:1], 0.0).then_inc(s_c, 1)
            pool.iota(rank[:, :], [[-1, E]], base=E, channel_multiplier=0,
                      allow_small_or_imprecise_dtypes=True).then_inc(s_c, 1)
            pool.iota(slot_no[:, :], [[1, SLOTS]], base=0, channel_multiplier=0,
                      allow_small_or_imprecise_dtypes=True).then_inc(s_c, 1)
            pool.wait_ge(s_c, 7)
            pool.affine_select(out=before[:, :], in_=before[:, :], compare_op=ALU.is_gt, fill=0.0, base=0,
                               pattern=[[1, P]], channel_multiplier=-1).then_inc(s_c, 1)

        @block.tensor
        def _(pe):
            pe.wait_ge(s_w, 32)
            for b in range(B):
                pe.wait_ge(s_z, b * KT + KT)
                for j in range(2):
                    for q in range(4):
                        mm = pe.transpose(ps_t[j][:, q * P:(q + 1) * P], z_all[:, b * KT + 4 * j + q, :], ident[:, :])
                    mm.then_inc(s_turn, 1)
                for j in range(2):
                    pe.wait_ge(s_zt, b * 2 + (j + 1))
                    for q in range(4):
                        t = b * KT + 4 * j + q
                        mm = pe.matmul(ps_logit[:, t * E:(t + 1) * E], zt[:, j, q * P:(q + 1) * P], w_r[:, :],
                                       start=True, stop=True)
                mm.then_inc(s_logit, 1)
            pe.wait_ge(s_chosen, 1)
            pe.wait_ge(s_c, 8)
            flat = chosen[:, :, :].rearrange("p t e -> p (t e)")
            pe.matmul(ps_before[:, :], before[:, :], flat, start=True, stop=True).then_inc(s_sum, 1)
            pe.matmul(ps_count[:, :], ones[:, :], flat, start=True, stop=True).then_inc(s_sum, 1)

        @block.scalar
        def _(act):
            with act.Fori(0, B) as b:
                for j in range(2):
                    act.wait_ge(s_turn, b * 2 + (j + 1))
                    act.activation(zt[:, j, :], ps_t[j][:, :], ACT.Copy).then_inc(s_zt, 1)
            act.wait_ge(s_shift, 1)
            act.activation(prob[:, :, :], logit[:, :, :], ACT.Exp).then_inc(s_exp, 1)

        @block.vector
        def _(dve):
            steps = [0]

            def step(instruction):
                steps[0] += 1
                instruction.then_inc(s_v, 1)
                dve.wait_ge(s_v, steps[0])

            def over_e(column):
                return column.unsqueeze(2).broadcast_to([P, TILES, E])

            with dve.Fori(0, B) as b:
                for k in range(KT):
                    normalise(dve, tile_of(z_all, b * KT + k), t_all, mv, rstd, b * KT + k).then_inc(s_z, 1)
            dve.wait_ge(s_w, 32)
            dve.wait_ge(s_c, 8)
            dve.wait_ge(s_logit, B)
            step(dve.tensor_tensor(work[:, :, :], ps_logit[:, :].rearrange("p (t e) -> p t e", e=E),
                                   b_r[:, :].unsqueeze(1).broadcast_to([P, TILES, E]), ALU.add))
            step(dve.tensor_reduce(col[0][:, :], work[:, :, :], AX.X, ALU.max))
            dve.tensor_tensor(logit[:, :, :], work[:, :, :], over_e(col[0][:, :]), ALU.subtract).then_inc(s_shift, 1)
            dve.wait_ge(s_exp, 1)
            step(dve.tensor_reduce(col[1][:, :], prob[:, :, :], AX.X, ALU.add))
            step(dve.reciprocal(col[2][:, :], col[1][:, :]))
            step(dve.tensor_tensor(work[:, :, :], prob[:, :, :], over_e(col[2][:, :]), ALU.mult))
            step(dve.tensor_reduce(col[3][:, :], work[:, :, :], AX.X, ALU.max))
            step(dve.reciprocal(col[4][:, :], col[3][:, :]))
            step(dve.tensor_tensor(gain[:, :], col[3][:, :], col[4][:, :], ALU.mult))
            step(dve.tensor_tensor(prob[:, :, :], work[:, :, :], over_e(col[3][:, :]), ALU.is_ge))
            step(dve.tensor_tensor(work[:, :, :], prob[:, :, :], rank[:, :].unsqueeze(1).broadcast_to([P, TILES, E]),
                                   ALU.mult))
            step(dve.tensor_reduce(col[5][:, :], work[:, :, :], AX.X, ALU.max))
            dve.tensor_tensor(chosen[:, :, :], work[:, :, :], over_e(col[5][:, :]), ALU.is_ge).then_inc(s_chosen, 1)
            dve.wait_ge(s_sum, 2)
            step(dve.tensor_copy(count[:, :, :], ps_count[:, :].rearrange("p (t e) -> p e t", e=E)))
            step(dve.tensor_tensor_scan(upto[:, :, :].rearrange("p e t -> p (e t)"),
                                        keep[:, :, :].rearrange("p e t -> p (e t)"),
                                        count[:, :, :].rearrange("p e t -> p (e t)"), 0.0, ALU.mult, ALU.add))
            step(dve.tensor_scalar(total_i[:, :], upto[:, :, TILES - 1], float(P - 1), None, ALU.add))
            step(dve.tensor_scalar(tiles_i[:, :], total_i[:, :], 7, None, ALU.arith_shift_right))
            step(dve.tensor_copy(tiles_e[:, :], tiles_i[:, :]))
            step(dve.tensor_tensor_scan(end_e[:, :], ones_e[:, :], tiles_e[:, :], 0.0, ALU.mult, ALU.add))
            step(dve.tensor_tensor(total[:, :], end_e[:, :], tiles_e[:, :], ALU.subtract))
            step(dve.tensor_scalar(base_e[:, :], total[:, :], float(P), None, ALU.mult))
            step(dve.tensor_tensor(upto[:, :, :], upto[:, :, :], count[:, :, :], ALU.subtract))
            step(dve.tensor_tensor(count[:, :, :], upto[:, :, :], base_e[:, :].unsqueeze(2).broadcast_to([P, E, TILES]),
                                   ALU.add))
            step(dve.tensor_tensor(upto[:, :, :], count[:, :, :], ps_before[:, :].rearrange("p (t e) -> p e t", e=E),
                                   ALU.add))
            step(dve.tensor_tensor(work[:, :, :], upto[:, :, :].rearrange("p e t -> p t e"), chosen[:, :, :], ALU.mult))
            step(dve.tensor_reduce(col[0][:, :], work[:, :, :], AX.X, ALU.add))
            step(dve.tensor_copy(pos[:, :], col[0][:, :]))
            step(dve.tensor_tensor(past[:, :, :], slot_no[:, :].unsqueeze(2).broadcast_to([P, SLOTS, E]),
                                   end_e[:, :].unsqueeze(1).broadcast_to([P, SLOTS, E]), ALU.is_ge))
            step(dve.tensor_reduce(slot_f[:, :], past[:, :, :], AX.X, ALU.add))
            step(dve.tensor_scalar(slot_expert[:, :], slot_f[:, :], float(E - 1), None, ALU.min))


def expert_kernel(nc, sb, psum, sem, w1, b1, w2, b2, z_all, t_all, ident, pos, slot_expert, gain, rows_in, rows_out, out):
    HC = HID // P
    w1_sb = sb("w1_sb", [P, E, HID], F32)
    w2_sb = sb("w2_sb", [P, E, HC, C], F32)
    b1_sb = sb("b1_sb", [P, E, HID], F32)
    b2_sb = sb("b2_sb", [P, E, C], F32)
    RING = 4
    x_in = sb("x_in", [P, RING, C], F32)
    xt = sb("xt", [P, 2, P], F32)
    hid_b = sb("hid_b", [P, 2, HID], F32)
    hid = sb("hid", [P, 2, HID], F32)
    hid_t = sb("hid_t", [P, 2, HID], F32)
    y = sb("y", [P, RING, C], F32)
    out_t = sb("out_t", [P, 2, HALF], F32)
    ps_x = [psum(f"ps_x{i}", [P, HALF], F32) for i in range(2)]
    ps_h = [psum(f"ps_h{i}", [P, HALF], F32) for i in range(2)]
    ps_t = [psum(f"ps_t{i}", [P, HALF], F32) for i in range(2)]
    ps_y = [psum(f"ps_y{i}", [P, HALF], F32) for i in range(2)]
    s_w = sem("e_w")
    s_sent = sem("e_sent")
    s_x = [sem(f"e_x{i}") for i in range(RING)]
    s_turn = sem("e_turn")
    s_xt = sem("e_xt")
    s_up = sem("e_up")
    s_bias = sem("e_bias")
    s_gelu = sem("e_gelu")
    s_ht = sem("e_ht")
    s_htc = sem("e_htc")
    s_down = sem("e_down")
    s_y = sem("e_y")
    s_st = [sem(f"e_st{i}") for i in range(RING)]
    s_back = [sem(f"e_back{i}") for i in range(B)]
    s_gain = sem("e_gain")
    s_add = sem("e_add")
    s_ot = sem("e_ot")
    s_oc = sem("e_oc")
    s_out = [sem(f"e_out{i}") for i in range(2)]
    AHEAD = 7
    assert (SLOTS - AHEAD) % RING == 0

    def rounds(i, n):
        return i + n // RING

    with nc.Block() as block:
        @block.sync
        def _(sp):
            sp.dma_start(w1_sb[:, :, :], w1.rearrange("e c h -> c e h")).then_inc(s_w, 16)
            sp.dma_start(w2_sb[:, :, :, :], w2.rearrange("e (k p) c -> p e k c", p=P)).then_inc(s_w, 16)
            sp.dma_start(b1_sb[:, :, :], b1.partition_broadcast(P)).then_inc(s_w, 16)
            sp.dma_start(b2_sb[:, :, :], b2.partition_broadcast(P)).then_inc(s_w, 16)

            def row(s):
                return s * P if isinstance(s, int) else sp.snap(s * P)

            def load(s, r, turned=None):
                first = row(s)
                if turned is not None:
                    sp.wait_ge(s_turn, turned)
                sp.dma_start(x_in[:, r, :], rows_in[bass.ds(first, P), :]).then_inc(s_x[r], 16)

            def store(s, r):
                first = row(s)
                sp.wait_ge(s_y, s + 1)
                sp.dma_start(rows_out[bass.ds(first, P), :], y[:, r, :]).then_inc(s_st[r], 16)

            sp.wait_ge(s_sent, 16 * TILES)
            for s in range(RING):
                load(s, s)

            for s in range(1, AHEAD):
                load(s + 3, (s + 3) % RING, s)
                store(s - 1, (s - 1) % RING)
            with sp.Fori(0, (SLOTS - AHEAD) // RING - 1) as i:
                for j in range(RING):
                    n = AHEAD + j
                    load(i * RING + (n + 3), (n + 3) % RING, i * RING + n)
                    store(i * RING + (n - 1), (n - 1) % RING)
            for s in range(SLOTS - RING, SLOTS):
                if s + 3 <= SLOTS:
                    load(s + 3, (s + 3) % RING, s)
                store(s - 1, (s - 1) % RING)
            store(SLOTS - 1, (SLOTS - 1) % RING)

            for b in range(B):
                for j in range(2):
                    sp.wait_ge(s_oc, 2 * b + j + 1)
                    sp.dma_start(out[b, :, j * HALF:(j + 1) * HALF], out_t[:, j, :]).then_inc(s_out[j], 16)
            for j in range(2):
                sp.wait_ge(s_out[j], 16 * B)

        @block.gpsimd
        def _(pool):
            for t in range(TILES):
                pool.indirect_dma_start(rows_in, bass.IndirectOffsetOnAxis(ap=pos[:, t:t + 1], axis=0),
                                        z_all[:, t, :], None).then_inc(s_sent, 16)
            for r in range(RING):
                pool.wait_ge(s_st[r], 16 * len(range(r, SLOTS, RING)))
            pool.wait_ge(s_sent, 16 * TILES)
            for t in range(TILES):
                pool.indirect_dma_start(z_all[:, t, :], None, rows_out,
                                        bass.IndirectOffsetOnAxis(ap=pos[:, t:t + 1], axis=0)).then_inc(s_back[t // KT], 16)

        @block.tensor
        def _(pe):
            def turn(s, n, i):
                pe.wait_ge(s_x[n % RING], rounds(i, n) * 16 + 16)
                if n >= 2:
                    pe.wait_ge(s_xt, s - 1)
                pe.transpose(ps_x[n % 2][:, 0:P], x_in[:, n % RING, :], ident[:, :]).then_inc(s_turn, 1)

            def up(s, n):
                e = pe.value_load(slot_expert[0:1, bass.ds(s, 1)], min_val=0, max_val=E - 1)
                pe.wait_ge(s_xt, s + 1)
                if n >= 2:
                    pe.wait_ge(s_bias, s - 1)
                pe.matmul(ps_h[n % 2][:, :], xt[:, n % 2, :], tile_of(w1_sb, e), start=True, stop=True).then_inc(s_up, 1)
                return e

            def hidden_turn(s, n):
                pe.wait_ge(s_gelu, s + 1)
                if n >= 2:
                    pe.wait_ge(s_htc, s - 1)
                for k in range(HC):
                    mm = pe.transpose(ps_t[n % 2][:, k * P:(k + 1) * P], hid[:, n % 2, k * P:(k + 1) * P], ident[:, :])
                mm.then_inc(s_ht, 1)

            def down(s, n, e):
                pe.wait_ge(s_htc, s + 1)
                if n >= 2:
                    pe.wait_ge(s_y, s - 1)
                w = w2_sb[:, bass.ds(e, 1), :, :].rearrange("p a k c -> p (a k) c")
                for k in range(HC):
                    mm = pe.matmul(ps_y[n % 2][:, 0:C], hid_t[:, n % 2, k * P:(k + 1) * P], w[:, k, :],
                                   start=(k == 0), stop=(k == HC - 1))
                mm.then_inc(s_down, 1)

            pe.wait_ge(s_w, 64)
            turn(0, 0, 0)
            up(0, 0)
            turn(1, 1, 0)

            def body(s, n, i):
                up(s, n)
                hidden_turn(s - 1, n - 1)
                turn(s + 1, n + 1, i)
                e = pe.value_load(slot_expert[0:1, bass.ds(s - 1, 1)], min_val=0, max_val=E - 1)
                down(s - 1, n - 1, e)

            for s in range(1, AHEAD):
                body(s, s, 0)
            with pe.Fori(0, (SLOTS - AHEAD) // RING) as i:
                for j in range(RING):
                    body(i * RING + (AHEAD + j), AHEAD + j, i)
            s = SLOTS - 1
            hidden_turn(s, s)
            down(s, s, pe.value_load(slot_expert[0:1, s:s + 1], min_val=0, max_val=E - 1))

            pe.wait_ge(s_xt, SLOTS + 1)
            for b in range(B):
                pe.wait_ge(s_add, KT * (b + 1))
                for j in range(2):
                    if b:
                        pe.wait_ge(s_oc, 2 * b + j - 1)
                    for q in range(4):
                        mm = pe.transpose(ps_x[j][:, q * P:(q + 1) * P], t_all[:, b * KT + 4 * j + q, :], ident[:, :])
                    mm.then_inc(s_ot, 1)

        @block.scalar
        def _(act):
            def copy_xt(s, n):
                act.wait_ge(s_turn, s + 1)
                if n >= 2:
                    act.wait_ge(s_up, s - 1)
                act.activation(xt[:, n % 2, :], ps_x[n % 2][:, 0:P], ACT.Copy).then_inc(s_xt, 1)

            def gelu(s, n):
                act.wait_ge(s_bias, s + 1)
                if n >= 2:
                    act.wait_ge(s_ht, s - 1)
                act.activation(hid[:, n % 2, :], hid_b[:, n % 2, :], ACT.Gelu).then_inc(s_gelu, 1)

            copy_xt(0, 0)
            copy_xt(1, 1)
            gelu(0, 0)

            def body(s, n):
                gelu(s, n)
                copy_xt(s + 1, n + 1)

            for s in range(1, AHEAD):
                body(s, s)
            with act.Fori(0, (SLOTS - AHEAD) // RING) as i:
                for j in range(RING):
                    body(i * RING + (AHEAD + j), AHEAD + j)

            for b in range(B):
                for j in range(2):
                    act.wait_ge(s_ot, 2 * b + j + 1)
                    if b:
                        act.wait_ge(s_out[j], 16 * b)
                    act.activation(out_t[:, j, :], ps_x[j][:, :], ACT.Copy).then_inc(s_oc, 1)

        @block.vector
        def _(dve):
            def bias(s, n):
                e = dve.value_load(slot_expert[0:1, bass.ds(s, 1)], min_val=0, max_val=E - 1)
                dve.wait_ge(s_up, s + 1)
                if n >= 2:
                    dve.wait_ge(s_gelu, s - 1)
                dve.tensor_tensor(hid_b[:, n % 2, :], ps_h[n % 2][:, :], tile_of(b1_sb, e), ALU.add).then_inc(s_bias, 1)

            def copy_ht(s, n):
                dve.wait_ge(s_ht, s + 1)
                if n >= 2:
                    dve.wait_ge(s_down, s - 1)
                dve.tensor_copy(hid_t[:, n % 2, :], ps_t[n % 2][:, :]).then_inc(s_htc, 1)

            def result(s, n, i):
                e = dve.value_load(slot_expert[0:1, bass.ds(s, 1)], min_val=0, max_val=E - 1)
                dve.wait_ge(s_down, s + 1)
                if n >= RING:
                    dve.wait_ge(s_st[n % RING], rounds(i, n) * 16)
                dve.tensor_tensor(y[:, n % RING, :], ps_y[n % 2][:, 0:C], tile_of(b2_sb, e), ALU.add).then_inc(s_y, 1)

            dve.wait_ge(s_w, 64)
            bias(0, 0)

            def body(s, n, i):
                bias(s, n)
                copy_ht(s - 1, n - 1)
                result(s - 1, n - 1, i)

            for s in range(1, AHEAD):
                body(s, s, 0)
            with dve.Fori(0, (SLOTS - AHEAD) // RING) as i:
                for j in range(RING):
                    body(i * RING + (AHEAD + j), AHEAD + j, i)
            s = SLOTS - 1
            copy_ht(s, s)
            result(s, s, 0)

            for t in range(TILES):
                dve.wait_ge(s_back[t // KT], 16 * KT)
                dve.scalar_tensor_tensor(out=t_all[:, t, :], in0=z_all[:, t, :], scalar=gain[:, t:t + 1],
                                         in1=t_all[:, t, :], op0=ALU.mult, op1=ALU.add).then_inc(s_add, 1)


def build(nc, x, w_proj, b_proj, w_out, b_out, wq, wk, wv, wr, br, w1, b1, w2, b2, out):
    rows_in = nc.dram_tensor("rows_in", [(SLOTS + 1) * P, C], F32).ap()
    rows_out = nc.dram_tensor("rows_out", [SLOTS * P, C], F32).ap()
    parts_dram = nc.dram_tensor("parts_dram", [2, 3, P, N], BF16).ap()

    def allocators(ctx):
        return (lambda n, s, d: ctx.enter_context(nc.sbuf_tensor(n, s, d)),
                lambda n, s, d: ctx.enter_context(nc.psum_tensor(n, s, d)),
                lambda n: ctx.enter_context(nc.semaphore(n)))

    with ExitStack() as top:
        sb, _, _ = allocators(top)
        t_all = sb("t_all", [P, TILES, C], F32)
        ident = sb("ident", [P, P], F32)
        identb = sb("identb", [P, P], BF16)
        with ExitStack() as ctx:
            attention_kernel(nc, *allocators(ctx), x, w_proj, b_proj, w_out, b_out, t_all, ident, identb, parts_dram)
        with ExitStack() as ctx:
            sb2, psum2, sem2 = allocators(ctx)
            mv, rstd = token_statistics(nc, sb2, sem2, t_all, "a")
            spike_kernel(nc, sb2, psum2, sem2, wq, wk, wv, t_all, mv, rstd, ident, rows_in)
        with ExitStack() as ctx:
            sb3, _, _ = allocators(ctx)
            z_all = sb3("z_all", [P, TILES, C], F32)
            pos = sb3("pos", [P, TILES], U32)
            slot_expert = sb3("slot_expert", [P, SLOTS], I32)
            gain = sb3("gain", [P, TILES], F32)
            with ExitStack() as ctx2:
                sb4, psum4, sem4 = allocators(ctx2)
                mv, rstd = token_statistics(nc, sb4, sem4, t_all, "b")
                routing_kernel(nc, sb4, psum4, sem4, wr, br, t_all, z_all, mv, rstd, ident, pos, slot_expert, gain)
            with ExitStack() as ctx2:
                expert_kernel(nc, *allocators(ctx2), w1, b1, w2, b2, z_all, t_all, ident, pos, slot_expert, gain,
                              rows_in, rows_out, out)


_INS = ['x', 'L0_conv_w_proj', 'L0_conv_b_proj', 'L0_conv_w_out', 'L0_conv_b_out', 'L1_attn_Wq', 'L1_attn_Wk',
        'L1_attn_Wv', 'L1_ffn_Wr', 'L1_ffn_br', 'L1_ffn_W1', 'L1_ffn_b1', 'L1_ffn_W2', 'L1_ffn_b2']


def kernel(**inputs):
    import numpy as _np
    import concourse.bacc as _bacc
    from concourse.bass_utils import run_bass_kernel_spmd as _run

    nc = _bacc.Bacc("TRN2", target_bir_lowering=False, num_devices=1)
    arrays, args = {}, []
    for name in _INS:
        a = _np.ascontiguousarray(inputs[name])
        if name == 'x':
            a = a.reshape(B, C, N)
        arrays[f"in_{name}"] = a
        args.append(nc.dram_tensor(f"in_{name}", a.shape, mybir.dt.from_np(a.dtype), kind="ExternalInput").ap())
    args.append(nc.dram_tensor("out_0", (B, C, N), F32, kind="ExternalOutput").ap())
    build(nc, *args)
    r = _run(nc, [arrays], core_ids=[0])
    return r.results[0]["out_0"].reshape(B, C, 32, 32)
```

```python
import concourse.bass as bass
from concourse import mybir
from contextlib import ExitStack

F32 = mybir.dt.float32
BF16 = mybir.dt.bfloat16
I32 = mybir.dt.int32
U32 = mybir.dt.uint32
ALU = mybir.AluOpType
ACT = mybir.ActivationFunctionType
AX = mybir.AxisListType

B, C, N = 8, 128, 1024
HEADS, DH = 8, 16
G = 2
HG = HEADS // G
GROWS = HG * DH
P = 128
KT = N // P
HALF = N // 2
TILES = B * KT
QK_SCALE = DH ** -0.5
Q_THRESH, K_THRESH, V_THRESH, MASK_THRESH = 0.25, 0.25, 0.3, 0.1
LN_EPS = 1e-5
E, HID = 8, 512
HC = HID // P
PORTIONS = (6, 2)
assert sum(PORTIONS) == B
SLOTS = sum(n * KT + E - 1 for n in PORTIONS)
SECOND = PORTIONS[0] * KT + E - 1


def portion(h):
    tiles = PORTIONS[h] * KT
    return PORTIONS[h], tiles, sum(PORTIONS[:h]) * KT, tiles + E - 1, h * SECOND


TERMS = [(0, 0), (0, 1), (0, 2), (1, 0), (1, 1), (2, 0)]
KROWS = DH * len(TERMS)
MROWS = 2
RUNS = [(0, 3), (1, 2), (2, 1)]
STACK_DMAS = len(TERMS) + len(RUNS)

BANKS_A = 6
ITEMS = KT * 2 * HG
KEYS = 2 * G
RING_KINDS = ("score", "v", "proj", "max", "mrow", "sums", "spread", "out")
V_AT, SUMS_AT, SPREAD_AT = 4, 8, (12, 16)
PROJ_AT, OUT_AT = (6, 10, 14, 18), (20, 24, 28, 32)
MAX_FROM, MAX_OVER, LAST_ROW_AT = 1, 57, 60
TAKE_AT, COMBINE_AT, KEEP_AT = (3, 0, 0), (3, 4, 0), (3, 6, 0)


def max_jobs():
    jobs = []
    for h in range(HG):
        for qt in range(KT):
            for half in range(2):
                jobs.append(("max", (h, qt, half)))
            if h and qt == 2:
                jobs += [("mrow", (h - 1, 0)), ("mrow", (h - 1, 1))]
    return jobs


LAST_ROW = [("mrow", (HG - 1, 0)), ("mrow", (HG - 1, 1))]


def finish_jobs(g):
    jobs = [(SUMS_AT, "sums", ()), (SPREAD_AT[0], "spread", (0,)), (SPREAD_AT[1], "spread", (1,))]
    if g == 1:
        jobs += [(OUT_AT[j], "out", (j,)) for j in range(4)]
    return jobs


def step_list(key, first=False, project=True, ahead=True):
    g = key % G
    side = []
    if not first:
        side += [(2, "last_pv", ())] + finish_jobs(1 - g)
    if ahead:
        side.append((V_AT, "v", ()))
        if g == 0 and project:
            side += [(PROJ_AT[n], "proj", (n // 2, n % 2)) for n in range(4)]
        jobs = max_jobs()
        side += [(MAX_FROM + n * MAX_OVER // len(jobs),) + job for n, job in enumerate(jobs)]
        side += [(LAST_ROW_AT,) + job for job in LAST_ROW]
    side.sort(key=lambda j: j[0])
    out = []
    for i in range(ITEMS):
        out.append((key, "score", (i,)))
        if i >= 6 and i % 4 == 2:
            out.append((key, "pv", ((i - 6) // 4,)))
        while side and side[0][0] <= i:
            out.append((key,) + side.pop(0)[1:])
    return out


def first_list():
    jobs = [("proj", (n // 2, n % 2)) for n in range(4)] + [("v", ())] + max_jobs() + LAST_ROW
    return [(3,) + job for job in jobs] + step_list(0, first=True)


def last_list():
    jobs = [("last_pv", ())] + [job[1:] for job in finish_jobs(1)]
    return step_list(3, ahead=False) + [(0,) + job for job in jobs]


START = first_list()
BODY = step_list(1) + step_list(2) + step_list(3) + step_list(0)
BEFORE_LAST = step_list(1) + step_list(2, project=False)
END = last_list()


def ring_uses(jobs):
    return sum(kind in RING_KINDS for _, kind, _ in jobs)


def use_of(jobs, key, kind, args=()):
    return ring_uses(jobs[:jobs.index((key, kind, args))])


LOOPS = B // 2 - 1
for step_jobs in (BODY, BEFORE_LAST):
    assert step_jobs.index((2, "out", (3,))) < step_jobs.index((2, "max", TAKE_AT))
R0, RB = ring_uses(START), ring_uses(BODY)
R_END = R0 + LOOPS * RB + ring_uses(BEFORE_LAST)
assert RB % BANKS_A == 0


def step_start(base, jobs, key):
    return base + ring_uses(jobs[:[job[0] for job in jobs].index(key)])


def numbers(i):
    return ({1: i * 4 + 1, 2: i * 4 + 2, 3: i * 4 + 3, 0: i * 4 + 4},
            {1: i * 2, 2: i * 2 + 1, 3: i * 2 + 1, 0: i * 2 + 2},
            {1: i, 2: i, 3: i, 0: i + 1})


def filled(b, n):
    return b * RB + (n + 1)


def emptied(b, n):
    return n % BANKS_A, b * (RB // BANKS_A) + (n // BANKS_A + 1)


def wait_emptied(eng, s_empty, b, uses):
    latest = {}
    for n in uses:
        if n >= 0:
            latest[n % BANKS_A] = max(n, latest.get(n % BANKS_A, -1))
    for n in latest.values():
        bank, count = emptied(b, n)
        eng.wait_ge(s_empty[bank], count)


def later(step):
    return not (isinstance(step, int) and step == 0)


def attention_kernel(nc, sb, psum, sem, x, w_proj, b_proj, w_out, b_out, t_all, stats, mv_batch, mv, ident,
                     identb, parts_dram):
    xp = [sb(f"xp{i}", [P, N], F32) for i in range(2)]
    xr = sb("xr", [P, N], F32)
    w_raw = [sb(f"w_raw{s}", [C, P], F32) for s in range(2)]
    w_qk = [sb(f"w_qk{s}", [C, P], F32) for s in range(2)]
    b_qk = [sb(f"b_qk{s}", [P, 1], F32) for s in range(2)]
    b_q = sb("b_q", [P, 1], F32)
    w_v = [sb(f"w_v{g}", [C, HG * DH], F32) for g in range(G)]
    b_v = [sb(f"b_v{g}", [P, HG * DH], F32) for g in range(G)]
    w_o = sb("w_o", [P, G, C], F32)
    b_o = sb("b_o", [P, C], F32)
    pick = sb("pick", [P, HG], F32)
    full = [[sb(f"full{s}{h}", [P, HALF], F32) for h in range(2)] for s in range(2)]
    rest = sb("rest", [P, HALF], F32)
    parts = [sb(f"parts{s}", [P, 3, N], BF16) for s in range(2)]
    stack = [[sb(f"stack{s}{k}", [P, HG, N], BF16) for k in range(KEYS)] for s in range(2)]
    v_sb = [sb(f"v_sb{g}", [P, KT, HG, 32], F32) for g in range(G)]
    probs = sb("probs", [P, 2, HG, N], F32)
    mx = sb("mx", [P, HG, KT, 2], F32)
    m_all = sb("m_all", [P, KT], F32)
    m_parts = sb("m_parts", [P, HG, KT, MROWS], BF16)
    o_sb = sb("o_sb", [P, 2, HALF], F32)
    inv = sb("inv", [P, KT, HG], F32)
    o_n = [sb(f"o_n{g}", [P, N], F32) for g in range(G)]

    ring = [psum(f"ring{i}", [P, HALF], F32) for i in range(BANKS_A)]
    outT = [psum(f"outT{i}", [P, HALF], F32) for i in range(2)]

    s_w = sem("s_w")
    s_wo = sem("s_wo")
    s_xp = [sem(f"s_xp{i}") for i in range(2)]
    s_xr = sem("s_xr")
    s_const = sem("s_const")
    s_rows = sem("s_rows")
    s_perm = sem("s_perm")
    s_fill = sem("s_fill")
    s_empty = [sem(f"s_empty{i}") for i in range(BANKS_A)]
    s_split = sem("s_split")
    s_parts = sem("s_parts")
    s_gp = sem("s_gp")
    s_dve = sem("s_dve")
    s_passed = sem("s_passed")
    s_stack = [sem(f"s_stack{k}") for k in range(KEYS)]
    s_mcol = sem("s_mcol")
    s_mm = sem("s_mm")
    s_pv = sem("s_pv")
    s_osb = sem("s_osb")
    s_stat = sem("s_stat")
    s_settled = sem("s_settled")

    def w_part(part):
        return w_proj.rearrange("c (h t) -> c h t", t=3 * DH)[:, :, part * DH:(part + 1) * DH]

    FIRST_NUMBERS = ({3: -1, 0: 0}, {3: -1, 0: 0}, {3: -1, 0: 0})
    W_DMAS = 2 * (1 + G) + 2 * G
    N_CONST = 1 + G + 3
    N_PERM = 3
    SUM_ROW = DH
    PARTS_DMAS = 2 * G

    def split_batch(eng, s_chain, chain, i, batch, jobs, key, settled):
        base = 0 if jobs is START else R0
        for n in range(4):
            s, half = n // 2, n % 2
            src, part = full[s][half], parts[s][:, :, half * HALF:(half + 1) * HALF]
            wait_emptied(eng, s_empty, i, [base + use_of(jobs, key, "proj", (s, half))])
            settled()
            eng.tensor_copy(part[:, 0, :], src[:, :]).then_inc(s_chain, 1)
            eng.wait_ge(s_chain, chain + (4 * n + 1))
            eng.tensor_tensor(rest[:, :], src[:, :], part[:, 0, :], ALU.subtract).then_inc(s_chain, 1)
            eng.wait_ge(s_chain, chain + (4 * n + 2))
            settled()
            eng.tensor_copy(part[:, 1, :], rest[:, :]).then_inc(s_chain, 1)
            eng.wait_ge(s_chain, chain + (4 * n + 3))
            eng.tensor_tensor(part[:, 2, :], rest[:, :], part[:, 1, :], ALU.subtract).then_inc(s_split, 1)
            eng.wait_ge(s_split, batch * 4 + (n + 1))
            eng.sem_inc(s_chain, 1)

    with nc.Block() as block:
        @block.sync
        def _(sp):
            sp.dma_start(xp[0][:, :], x[0]).then_inc(s_xp[0], 16)
            b_parts = b_proj.rearrange("(g h t d) -> t g d h", g=G, h=HG, t=3)
            for s in range(2):
                sp.dma_start(w_raw[s][:, :].rearrange("c (h d) -> c h d", d=DH), w_part(s)).then_inc(s_w, 16)
                for g in range(G):
                    sp.dma_start(b_qk[s][g * HG * DH:(g + 1) * HG * DH, :], b_parts[s, g].unsqueeze(2),
                                 allow_slow_non_contiguous=True).then_inc(s_w, 16)
            for g in range(G):
                heads = slice(g * HG, (g + 1) * HG)
                sp.dma_start(w_v[g][:, :].rearrange("c (h d) -> c h d", d=DH), w_part(2)[:, heads, :]).then_inc(s_w, 16)
                sp.dma_start(b_v[g][:, :].rearrange("p (h d) -> p h d", d=DH),
                             b_proj.rearrange("(h t d) -> t h d", h=HEADS, t=3)[2, heads].partition_broadcast(P)
                             ).then_inc(s_w, 16)
            sp.dma_start(xp[1][:, :], x[1]).then_inc(s_xp[1], 16)
            sp.dma_start(xr[:, :], x[0]).then_inc(s_xr, 16)

            def put_parts():
                for s in range(2):
                    for g in range(G):
                        sp.dma_start(parts_dram[s, g].rearrange("c r n -> r c n"),
                                     parts[s][g * GROWS:(g + 1) * GROWS, :, :]).then_inc(s_parts, 16)

            def stack_up(key):
                g, row = key % G, 0
                for c, count in RUNS:
                    rows = slice(row, row + count * DH)
                    sp.dma_start(stack[1][key][rows, :, :].rearrange("r h n -> r (h n)"),
                                 parts_dram[1, g, 0:count].rearrange("c (d h) n -> (c d) (h n)", d=DH)
                                 ).then_inc(s_stack[key], 16)
                    for n in range(count):
                        sp.dma_start(stack[0][key][row:row + DH, :, :].rearrange("r h n -> r (h n)"),
                                     parts_dram[0, g, c].rearrange("(d h) n -> d (h n)", d=DH)
                                     ).then_inc(s_stack[key], 16)
                        row += DH

            sp.wait_ge(s_split, 4)
            put_parts()
            sp.wait_ge(s_parts, 16 * PARTS_DMAS)
            for key in (0, 1):
                stack_up(key)
            sp.dma_start(b_o[:, :], b_out.partition_broadcast(P)).then_inc(s_wo, 16)
            sp.wait_ge(s_const, N_CONST)
            for g in range(G):
                for h in range(HG):
                    r = (g * HG + h) * DH
                    sp.dma_start(w_o[32 * h:32 * h + DH, g, :], w_out[r:r + DH, :]).then_inc(s_wo, 16)

            def next_parts(batches, pair):
                sp.wait_ge(s_split, batches * 4)
                put_parts()
                sp.wait_ge(s_parts, batches * (16 * PARTS_DMAS))
                for key in (pair, pair + 1):
                    stack_up(key)

            for key in (0, 1):
                sp.wait_ge(s_stack[key], 16 * STACK_DMAS)
            next_parts(2, 2)

            def batch(i, jobs, more):
                def done(key, kind, args=()):
                    sp.wait_ge(s_fill, filled(i, R0 + use_of(jobs, key, kind, args)))

                if more:
                    sp.wait_ge(s_fill, i * RB + R0)
                    sp.dma_start(xp[0][:, :], x[i * 2 + 2]).then_inc(s_xp[0], 16)
                    done(2, "v")
                    sp.dma_start(xp[1][:, :], x[i * 2 + 3]).then_inc(s_xp[1], 16)
                if more:
                    next_parts(i * 2 + 3, 0)
                done(2, "out", (3,))
                sp.dma_start(xr[:, :], x[i * 2 + 1]).then_inc(s_xr, 16)
                if more:
                    next_parts(i * 2 + 4, 2)
                    done(0, "out", (3,))
                    sp.dma_start(xr[:, :], x[i * 2 + 2]).then_inc(s_xr, 16)

            with sp.Fori(0, LOOPS) as i:
                batch(i, BODY, True)
            batch(LOOPS, BEFORE_LAST, False)

        @block.gpsimd
        def _(pool):
            pool.memset(ident[:, :], 0.0).then_inc(s_gp, 1)
            pool.memset(identb[:, :], 0.0).then_inc(s_gp, 1)
            pool.memset(pick[:, :], 0.0).then_inc(s_gp, 1)
            pool.wait_ge(s_gp, 3)
            for m in (ident, identb):
                pool.affine_select(out=m[:, :], in_=m[:, :], compare_op=ALU.not_equal, fill=1.0, base=0,
                                   pattern=[[-1, P]], channel_multiplier=1).then_inc(s_const, 1)
            pool.affine_select(out=pick[:, :], in_=pick[:, :], compare_op=ALU.not_equal, fill=1.0, base=-SUM_ROW,
                               pattern=[[-32, HG]], channel_multiplier=1).then_inc(s_const, 1)
            for g in range(G):
                pool.memset(v_sb[g][:, :, :, DH:32], 1.0).then_inc(s_const, 1)
            pool.memset(w_o[:, :, :], 0.0).then_inc(s_const, 1)
            pool.wait_ge(s_const, N_CONST)
            for key in range(KEYS):
                pool.memset(stack[1][key][KROWS:KROWS + MROWS, :, :], 1.0).then_inc(s_rows, 1)
            pool.wait_ge(s_rows, KEYS)

            def settled():
                pool.sem_inc(s_passed, 1)

            pool.wait_ge(s_parts, 16 * PARTS_DMAS)
            split_batch(pool, s_gp, 3, 0, 1, START, 0, settled)
            with pool.Fori(0, LOOPS) as i:
                for n, key in enumerate((2, 0)):
                    pool.wait_ge(s_parts, (i * 2 + (2 + n)) * (16 * PARTS_DMAS))
                    split_batch(pool, s_gp, i * 32 + (19 + 16 * n), i, i * 2 + (2 + n), BODY, key, settled)

        @block.tensor
        def _(pe):
            def run(i, base, jobs, steps):
                step_of, batch_of, pair_of = steps
                n = base
                rows = [base - BANKS_A, base - BANKS_A + 1] if base else []
                for key, kind, args in jobs:
                    g, nxt = key % G, (key + 1) % KEYS
                    if kind in ("pv", "last_pv"):
                        own = kind == "pv"
                        j, gg, step = (args[0], g, step_of[key]) if own else (15, 1 - g, step_of[key] - 1)
                        kt, half = j // 2, j % 2
                        wait_emptied(pe, s_empty, i, [base + use_of(jobs, key, "score", (4 * j + 3,)) if own
                                                      else step_start(base, jobs, key) - 1])
                        if kt == 0 and later(step):
                            pe.wait_ge(s_osb, step * 2 + (half - 1))
                        for h in range(HG):
                            mm = pe.matmul(outT[half][32 * h:32 * h + 32, :], v_sb[gg][:, kt, h, :],
                                           probs[:, kt % 2, h, half * HALF:(half + 1) * HALF],
                                           start=(kt == 0), stop=(kt == KT - 1))
                        mm.then_inc(s_pv, 1)
                        continue
                    needs = [n - BANKS_A]
                    if kind == "mrow":
                        rows = rows[-1:] + [n]
                    if kind == "score" and args[0] == 0:
                        needs += rows
                    if kind == "spread":
                        needs.append(base + use_of(jobs, key, "sums"))
                    if kind == "out":
                        needs.append(base + use_of(jobs, key, "spread", (args[0] // 2,)))
                    wait_emptied(pe, s_empty, i, needs)
                    if kind == "score" and base == 0 and args[0] == 0:
                        pe.wait_ge(s_rows, KEYS)
                    out = ring[n % BANKS_A]
                    if kind == "score":
                        kt, half, h = args[0] // 8, args[0] // 4 % 2, args[0] % 4
                        mm = pe.matmul(out[:, :], stack[1][key][0:KROWS + MROWS, h, kt * P:(kt + 1) * P],
                                       stack[0][key][0:KROWS + MROWS, h, half * HALF:(half + 1) * HALF],
                                       start=True, stop=True)
                    elif kind == "proj":
                        s, half = args
                        odd = key // 2
                        if args == (0, 0):
                            pe.wait_ge(s_xp[1 - odd], pair_of[key] * 16 + (16 + 16 * odd))
                        mm = pe.matmul(out[:, :], w_qk[s][:, :], xp[1 - odd][:, half * HALF:(half + 1) * HALF],
                                       start=True, stop=True)
                    elif kind == "v":
                        for kt in range(KT):
                            mm = pe.matmul(out[:, kt * 64:(kt + 1) * 64], xp[nxt // 2][:, kt * P:(kt + 1) * P],
                                           w_v[nxt % G][:, :], start=True, stop=True)
                    elif kind == "max":
                        h, qt, half = args
                        if args == (0, 0, 0):
                            pe.wait_ge(s_stack[nxt], (pair_of[key] + (2 if key == 3 else 1)) * (16 * STACK_DMAS))
                        mm = pe.matmul(out[:, :], stack[0][nxt][0:KROWS, h, qt * P:(qt + 1) * P],
                                       stack[1][nxt][0:KROWS, h, half * HALF:(half + 1) * HALF], start=True, stop=True)
                    elif kind == "mrow":
                        h, half = args
                        if half == 0:
                            pe.wait_ge(s_mm, step_of[key] * HG + (HG + h + 1))
                        for q in range(KT // 2):
                            mm = pe.matmul(out[KROWS:KROWS + MROWS, q * P:(q + 1) * P],
                                           m_parts[:, h, half * (KT // 2) + q, :], identb[:, :], start=True, stop=True)
                    elif kind == "sums":
                        pe.wait_ge(s_osb, step_of[key] * 2)
                        for q in range(KT):
                            mm = pe.matmul(out[:, q * HG:(q + 1) * HG],
                                           o_sb[:, q // 4, q % 4 * P:(q % 4 + 1) * P], pick[:, :], start=True, stop=True)
                    elif kind == "spread":
                        for q in range(KT // 2):
                            for h in range(HG):
                                mm = pe.matmul(out[32 * h:32 * h + 32, q * P:(q + 1) * P],
                                               inv[:, args[0] * 4 + q, h:h + 1].broadcast_to([P, 32]),
                                               ident[:, :], start=True, stop=True)
                    elif kind == "out":
                        if args[0] == 0:
                            pe.wait_ge(s_xr, batch_of[key] * 16)
                        for q in range(2):
                            tok = slice((args[0] * 2 + q) * P, (args[0] * 2 + q + 1) * P)
                            dst = out[:, q * C:(q + 1) * C]
                            pe.matmul(dst, o_n[0][:, tok], w_o[:, 0, :], start=True, stop=False)
                            pe.matmul(dst, o_n[1][:, tok], w_o[:, 1, :], start=False, stop=False)
                            mm = pe.matmul(dst, xr[:, tok], ident[:, :], start=False, stop=True)
                    mm.then_inc(s_fill, 1)
                    n += 1

            pe.sem_inc(s_pv, 4)
            pe.wait_ge(s_w, 16 * W_DMAS)
            pe.wait_ge(s_perm, N_PERM)
            pe.wait_ge(s_const, N_CONST)
            run(0, 0, START, FIRST_NUMBERS)
            pe.wait_ge(s_wo, 16 * (1 + HEADS))
            with pe.Fori(0, LOOPS) as i:
                run(i, R0, BODY, numbers(i))
            run(LOOPS, R0, BEFORE_LAST, numbers(LOOPS))
            run(0, R_END, END, numbers(LOOPS))

        @block.scalar
        def _(act):
            def copy_out(step, half):
                act.wait_ge(s_pv, step * 16 + (3 + half))
                act.activation(o_sb[:, half, :], outT[half][:, :], ACT.Copy).then_inc(s_osb, 1)

            def run(i, base, jobs, steps):
                step_of, batch_of, _ = steps
                n = base - 1
                for key, kind, args in jobs:
                    if kind not in RING_KINDS:
                        continue
                    n += 1
                    if kind not in ("score", "mrow", "proj"):
                        continue
                    bank, _ = emptied(i, n)
                    if kind == "score" and args[0] % 4 == 0:
                        act.wait_ge(s_pv, step_of[key] * 16 + (args[0] // 4 + 1))
                    if kind == "proj" and jobs.index((key, kind, args)) > 4:
                        act.wait_ge(s_split, batch_of[key] * 4 + 4)
                    act.wait_ge(s_fill, filled(i, n))
                    ps = ring[bank]
                    if kind == "score":
                        kt, half, h = args[0] // 8, args[0] // 4 % 2, args[0] % 4
                        act.activation(probs[:, kt % 2, h, half * HALF:(half + 1) * HALF], ps[:, :],
                                       ACT.Exp).then_inc(s_empty[bank], 1)
                        if args[0] in (1, 4) and later(step_of[key]):
                            copy_out(step_of[key], args[0] // 4)
                    elif kind == "mrow":
                        h, half = args
                        act.activation(stack[0][(key + 1) % KEYS][KROWS:KROWS + MROWS, h, half * HALF:(half + 1) * HALF],
                                       ps[KROWS:KROWS + MROWS, :], ACT.Copy).then_inc(s_empty[bank], 1)
                    elif kind == "proj":
                        s, half = args
                        act.activation(full[s][half][:, :], ps[:, :], ACT.Identity,
                                       bias=(b_q if s == 0 else b_qk[1])[:, 0:1],
                                       scale=QK_SCALE if s == 0 else 1.0).then_inc(s_empty[bank], 1)

            act.wait_ge(s_perm, N_PERM)
            run(0, 0, START, FIRST_NUMBERS)
            with act.Fori(0, LOOPS) as i:
                run(i, R0, BODY, numbers(i))
            run(LOOPS, R0, BEFORE_LAST, numbers(LOOPS))
            run(0, R_END, END, numbers(LOOPS))
            for half in range(2):
                copy_out(2 * B, half)

        @block.vector
        def _(dve):
            def take(b):
                dve.sem_inc(s_settled, 1)
                for k in range(KT):
                    last = dve.bn_stats(stats[:, k, :], tile_of(t_all, b * KT + k))
                last.then_inc(s_stat, 1)

            def combine(b):
                dve.wait_ge(s_stat, b * 3 + 1)
                dve.sem_inc(s_settled, 1)
                for k in range(KT):
                    last = dve.bn_aggr(mv_batch[:, k, :], stats[:, k, :])
                last.then_inc(s_stat, 1)

            def keep(b):
                dve.wait_ge(s_stat, b * 3 + 2)
                dve.tensor_copy(mv[:, bass.ds(b * KT, KT), :], mv_batch[:, :, :]).then_inc(s_stat, 1)

            def run(i, base, jobs, steps):
                step_of, batch_of, _ = steps
                n, before, out_use = base - 1, None, None
                for key, kind, args in jobs:
                    g = key % G
                    if kind == "v" and jobs.index((key, kind, args)) == 4:
                        split_batch(dve, s_dve, 0, 0, 0, START, 3, lambda: None)
                    if kind not in RING_KINDS:
                        continue
                    n += 1
                    if kind not in ("v", "max", "sums", "spread", "out"):
                        continue
                    bank, _ = emptied(i, n)
                    dve.wait_ge(s_fill, filled(i, n))
                    ps = ring[bank]
                    if kind == "v":
                        gg = (key + 1) % G
                        dve.tensor_tensor(v_sb[gg][:, :, :, 0:DH],
                                          ps[:, :].rearrange("p (k h d) -> p k h d", k=KT, d=DH),
                                          b_v[gg][:, :].rearrange("p (h d) -> p h d", d=DH).unsqueeze(1)
                                          .broadcast_to([P, KT, HG, DH]), ALU.add).then_inc(s_empty[bank], 1)
                    elif kind == "max":
                        h, qt, half = args
                        dve.tensor_reduce(mx[:, h, qt, half:half + 1], ps[:, :], AX.X,
                                          ALU.max).then_inc(s_empty[bank], 1)
                        if qt == KT - 1 and half == 1:
                            done = step_of[key] * HG + (HG + h)
                            wait_emptied(dve, s_empty, i, [before, n])
                            dve.tensor_reduce(m_all[:, :], mx[:, h, :, :], AX.X, ALU.max).then_inc(s_mcol, 1)
                            dve.wait_ge(s_mcol, done * 2 + 1)
                            dve.tensor_scalar(m_parts[:, h, :, 0], m_all[:, :], -1.0, None,
                                              ALU.mult).then_inc(s_mcol, 1)
                            dve.wait_ge(s_mcol, done * 2 + 2)
                            dve.scalar_tensor_tensor(out=m_parts[:, h, :, 1], in0=m_all[:, :], scalar=-1.0,
                                                     in1=m_parts[:, h, :, 0], op0=ALU.mult,
                                                     op1=ALU.subtract).then_inc(s_mm, 1)
                            dve.wait_ge(s_mm, done + 1)
                        before = n
                        if g == 0 and later(step_of[key]) and args == TAKE_AT:
                            wait_emptied(dve, s_empty, i, [out_use])
                            take(batch_of[key] - 1)
                        if g == 0 and later(step_of[key]) and args == COMBINE_AT:
                            combine(batch_of[key] - 1)
                        if g == 0 and later(step_of[key]) and args == KEEP_AT:
                            keep(batch_of[key] - 1)
                    elif kind == "sums":
                        dve.reciprocal(inv[:, :, :], ps[:, 0:KT * HG].rearrange("p (k h) -> p k h", h=HG)
                                       ).then_inc(s_empty[bank], 1)
                    elif kind == "spread":
                        half = args[0]
                        dve.tensor_tensor(o_n[(key + 1) % G][:, half * HALF:(half + 1) * HALF], o_sb[:, half, :], ps[:, :],
                                          ALU.mult).then_inc(s_empty[bank], 1)
                    elif kind == "out":
                        out_use = n
                        first = batch_of[key] * KT + (args[0] * 2 - KT)
                        dve.tensor_tensor(t_all[:, bass.ds(first, 2), :],
                                          ps[:, 0:2 * C].rearrange("p (q c) -> p q c", c=C),
                                          b_o[:, :].unsqueeze(1).broadcast_to([P, 2, C]),
                                          ALU.add).then_inc(s_empty[bank], 1)

            dve.wait_ge(s_w, 16 * W_DMAS)
            for s in range(2):
                dve.tensor_copy(w_qk[s][:, :].rearrange("c (g d h) -> c g h d", g=G, d=DH),
                                w_raw[s][:, :].rearrange("c (g h d) -> c g h d", g=G, d=DH)).then_inc(s_perm, 1)
            dve.tensor_scalar(b_q[:, :], b_qk[0][:, :], QK_SCALE, None, ALU.mult).then_inc(s_perm, 1)
            dve.wait_ge(s_const, N_CONST)
            run(0, 0, START, FIRST_NUMBERS)
            dve.wait_ge(s_wo, 16 * (1 + HEADS))
            with dve.Fori(0, LOOPS) as i:
                run(i, R0, BODY, numbers(i))
            run(LOOPS, R0, BEFORE_LAST, numbers(LOOPS))
            run(0, R_END, END, numbers(LOOPS))
            wait_emptied(dve, s_empty, 0, [R_END + ring_uses(END) - 1])
            take(B - 1)
            combine(B - 1)
            keep(B - 1)


def tile_of(ap, n):
    return ap[:, bass.ds(n, 1), :].rearrange("p a s -> p (a s)")


def variances(dve, mv, std, h, s_var):
    _, HT, T0, _, _ = portion(h)
    dve.tensor_scalar(std[:, :], mv[:, T0:T0 + HT, 1], LN_EPS, None, ALU.add).then_inc(s_var, 1)


def roots(act, std, s_var, s_std):
    act.wait_ge(s_var, 1)
    act.activation(std[:, :], std[:, :], ACT.Sqrt).then_inc(s_std, 1)


def inverses(dve, std, rstd, s_std, s_rstd):
    dve.wait_ge(s_std, 1)
    dve.reciprocal(rstd[:, :], std[:, :]).then_inc(s_rstd, 1)


def normalise(eng, out, t_all, mv, rstd, h, n):
    _, _, T0, _, _ = portion(h)
    return eng.tensor_scalar(out, tile_of(t_all, n + T0), mv[:, bass.ds(n + T0, 1), 0],
                             rstd[:, bass.ds(n, 1)], ALU.subtract, ALU.mult)


BANKS = 8
MASKS = [(m, lo, min(lo + HALF, N)) for m in range(KT) for lo in range(m * P, N, HALF)]
TURN_SPIKE = [("turn", (j,)) for j in range(2)] + [("spike", (s, half)) for s in range(2) for half in range(2)]
SPIKE_V = [("spike_v", (j,)) for j in range(2)]
COUNT = [("count", (j,)) for j in range(4)]
MASK = [("mask", m) for m in MASKS]
SPIKE_FIRST = TURN_SPIKE + SPIKE_V
SPIKE_BODY = MASK + TURN_SPIKE + COUNT + SPIKE_V
SPIKE_LAST = MASK + COUNT
assert len(SPIKE_FIRST) == BANKS and len(SPIKE_BODY) % BANKS == 0


def has_diagonal(args):
    m, lo, _ = args
    return lo == m * P


def spike_use(b, n):
    return n % BANKS, b * (len(SPIKE_BODY) // BANKS) + (BANKS + n) // BANKS


def spike_kernel(nc, sb, psum, sem, h, w_t, wq, wk, wv, t_all, mv, stats, mv_batch, mv_b, ident, sync_too, gpsimd_too):
    HB, HT, T0, _, _ = portion(h)
    std = sb("std", [P, HT], F32)
    rstd = sb("rstd", [P, HT], F32)
    w_raw = sb("w_raw", [P, 3, C], F32)
    z = sb("z", [P, KT, C], F32)
    zt = sb("zt", [P, N], F32)
    spikes = [sb(f"spikes{s}", [P, N], BF16) for s in range(2)]
    spikes_v = sb("spikes_v", [P, KT, C], BF16)
    mask = sb("mask", [P, KT, N], BF16)
    causal = sb("causal", [P, P], BF16)
    bank = [psum(f"bank{i}", [P, HALF], F32) for i in range(BANKS)]
    s_w = sem("sp_w")
    s_c = sem("sp_c")
    s_wt = sem("sp_wt")
    s_wc = sem("sp_wc")
    s_z = sem("sp_z")
    s_var = sem("sp_var")
    s_std = sem("sp_std")
    s_rstd = sem("sp_rstd")
    s_stat = sem("sp_stat")
    s_settled = sem("sp_settled")
    s_fill = sem("sp_fill")
    s_empty = [sem(f"sp_empty{i}") for i in range(BANKS)]

    with nc.Block() as block:
        @block.sync
        def _(sp):
            if h == 0:
                for n, w in enumerate((wq, wk, wv)):
                    sp.dma_start(w_raw[:, n, :], w).then_inc(s_w, 16)
            sync_too(sp)

        @block.gpsimd
        def _(pool):
            pool.memset(causal[:, :], 1.0).then_inc(s_c, 1)
            pool.wait_ge(s_c, 1)
            pool.affine_select(out=causal[:, :], in_=causal[:, :], compare_op=ALU.is_ge, fill=0.0, base=0,
                               pattern=[[1, P]], channel_multiplier=-1).then_inc(s_c, 1)
            gpsimd_too(pool)
            if h == 0:
                pool.wait_ge(s_rstd, 1)
                for b in range(1, HB):
                    pool.wait_ge(s_fill, 2 if b == 1 else (b - 2) * len(SPIKE_BODY) + BANKS + len(MASKS) + 2)
                    for k in range(KT):
                        normalise(pool, z[:, k, :], t_all, mv, rstd, h, b * KT + k).then_inc(s_z, 1)

        @block.tensor
        def _(pe):
            if h == 0:
                pe.wait_ge(s_w, 48)
                for n in range(3):
                    mm = pe.transpose(bank[0][:, n * C:(n + 1) * C], w_raw[:, n, :], ident[:, :])
                mm.then_inc(s_wt, 1)
                pe.wait_ge(s_wc, 1)

            def use(b, n, kind, args, tiles):
                i, emptied = spike_use(b, n)
                out = bank[i]
                if kind == "mask" and args[0] == 0 and args[1] == 0:
                    for back in range(1, BANKS + 1):
                        j, before = spike_use(b, n - back)
                        pe.wait_ge(s_empty[j], before + 1)
                elif kind == "count" and args[0] == 0:
                    for m in range(n - BANKS, len(MASKS)):
                        j, before = spike_use(b, m)
                        pe.wait_ge(s_empty[j], before + 1)
                elif b is not None and not (n < 0):
                    pe.wait_ge(s_empty[i], emptied)
                if kind == "turn":
                    pe.wait_ge(s_z, tiles)
                    for q in range(4):
                        mm = pe.transpose(out[:, q * P:(q + 1) * P], z[:, args[0] * 4 + q, :], ident[:, :])
                elif kind == "spike":
                    s, half = args
                    if s == 0:
                        j, before = spike_use(b, n - 2)
                        pe.wait_ge(s_empty[j], before + 1)
                    mm = pe.matmul(out[:, :], w_t[:, s, :], zt[:, half * HALF:(half + 1) * HALF], start=True, stop=True)
                elif kind == "spike_v":
                    for q in range(4):
                        tok = args[0] * 4 + q
                        mm = pe.matmul(out[:, q * C:(q + 1) * C], zt[:, tok * P:(tok + 1) * P], w_t[:, 2, :],
                                       start=True, stop=True)
                elif kind == "mask":
                    m, lo, hi = args
                    mm = pe.matmul(out[:, 0:hi - lo], spikes[1][:, m * P:(m + 1) * P], spikes[0][:, lo:hi],
                                   start=True, stop=True)
                elif kind == "count":
                    for q in range(2):
                        l = args[0] * 2 + q
                        for m in range(l + 1):
                            mm = pe.matmul(out[:, q * C:(q + 1) * C], mask[:, m, l * P:(l + 1) * P],
                                           spikes_v[:, m, :], start=(m == 0), stop=(m == l))
                mm.then_inc(s_fill, 1)

            for n, (kind, args) in enumerate(SPIKE_FIRST):
                use(0, n - BANKS, kind, args, KT)
            with pe.Fori(0, HB - 1) as b:
                for n, (kind, args) in enumerate(SPIKE_BODY):
                    use(b, n, kind, args, b * KT + 2 * KT)
            for n, (kind, args) in enumerate(SPIKE_LAST):
                use(HB - 1, n, kind, args, 0)

        @block.scalar
        def _(act):
            if h == 0:
                act.wait_ge(s_wt, 1)
                act.activation(w_t[:, :, :], bank[0][:, 0:3 * C].rearrange("p (n c) -> p n c", n=3),
                               ACT.Copy).then_inc(s_wc, 1)

            def turned(b, n, j):
                i, _ = spike_use(b, n)
                act.wait_ge(s_fill, b * len(SPIKE_BODY) + (BANKS + n + 1))
                act.activation(zt[:, j * HALF:(j + 1) * HALF], bank[i][:, :], ACT.Copy).then_inc(s_empty[i], 1)

            def masked(b, n, m, lo, hi):
                i, _ = spike_use(b, n)
                act.wait_ge(s_fill, b * len(SPIKE_BODY) + (BANKS + n + 1))
                act.activation(mask[:, m, lo:hi], bank[i][:, 0:hi - lo], ACT.Sign).then_inc(s_empty[i], 1)

            def masks(b):
                for n, args in enumerate(MASKS):
                    if not has_diagonal(args):
                        masked(b, n, *args)

            roots(act, std, s_var, s_std)
            for j in range(2):
                turned(0, j - BANKS, j)
            with act.Fori(0, HB - 1) as b:
                masks(b)
                for j in range(2):
                    turned(b, len(MASKS) + j, j)
            masks(HB - 1)

        @block.vector
        def _(dve):
            def statistics(b, counted):
                i, emptied = spike_use(b, counted)
                dve.wait_ge(s_empty[i], emptied + 1)
                dve.sem_inc(s_settled, 1)
                for k in range(KT):
                    last = dve.bn_stats(stats[:, k, :], tile_of(t_all, b * KT + (T0 + k)))
                last.then_inc(s_stat, 1)
                dve.wait_ge(s_stat, b * 3 + 1)
                dve.sem_inc(s_settled, 1)
                for k in range(KT):
                    last = dve.bn_aggr(mv_batch[:, k, :], stats[:, k, :])
                last.then_inc(s_stat, 1)
                dve.wait_ge(s_stat, b * 3 + 2)
                dve.tensor_copy(mv_b[:, bass.ds(b * KT + T0, KT), :], mv_batch[:, :, :]).then_inc(s_stat, 1)

            def use(b, n, kind, args):
                i, _ = spike_use(b, n)
                if kind == "turn" or (kind == "mask" and not has_diagonal(args)):
                    return
                dve.wait_ge(s_fill, b * len(SPIKE_BODY) + (BANKS + n + 1))
                ps = bank[i]
                if kind == "spike":
                    s, half = args
                    dve.tensor_scalar(spikes[s][:, half * HALF:(half + 1) * HALF], ps[:, :], (Q_THRESH, K_THRESH)[s],
                                      None, ALU.is_ge).then_inc(s_empty[i], 1)
                elif kind == "spike_v":
                    dve.tensor_scalar(spikes_v[:, args[0] * 4:args[0] * 4 + 4, :],
                                      ps[:, :].rearrange("p (q c) -> p q c", c=C), V_THRESH, None,
                                      ALU.is_ge).then_inc(s_empty[i], 1)
                elif kind == "mask":
                    m, lo, hi = args
                    last = dve.scalar_tensor_tensor(out=mask[:, m, lo:lo + P], in0=ps[:, 0:P], scalar=MASK_THRESH,
                                                    in1=causal[:, :], op0=ALU.is_gt, op1=ALU.mult)
                    if lo + P < hi:
                        last = dve.tensor_scalar(mask[:, m, lo + P:hi], ps[:, P:hi - lo], MASK_THRESH, None, ALU.is_gt)
                    last.then_inc(s_empty[i], 1)
                elif kind == "count":
                    tiles = t_all[:, bass.ds(b * KT + (T0 + args[0] * 2), 2), :]
                    dve.tensor_tensor(tiles, tiles, ps[:, 0:2 * C].rearrange("p (q c) -> p q c", c=C),
                                      ALU.add).then_inc(s_empty[i], 1)

            variances(dve, mv, std, h, s_var)
            inverses(dve, std, rstd, s_std, s_rstd)
            dve.wait_ge(s_rstd, 1)
            for k in range(KT):
                normalise(dve, z[:, k, :], t_all, mv, rstd, h, k).then_inc(s_z, 1)
            dve.wait_ge(s_c, 2)
            for n, (kind, args) in enumerate(SPIKE_FIRST):
                use(0, n - BANKS, kind, args)
            with dve.Fori(0, HB - 1) as b:
                if h:
                    for k in range(KT):
                        normalise(dve, z[:, k, :], t_all, mv, rstd, h, b * KT + (KT + k)).then_inc(s_z, 1)
                for n, (kind, args) in enumerate(SPIKE_BODY):
                    use(b, n, kind, args)
                statistics(b, len(MASKS) + len(TURN_SPIKE) + len(COUNT) - 1)
            for n, (kind, args) in enumerate(SPIKE_LAST):
                use(HB - 1, n, kind, args)
            statistics(HB - 1, len(SPIKE_LAST) - 1)


def routing_kernel(nc, sb, psum, sem, h, wr, br, t_all, z_all, mv, ident, pos, pos_out, slot_expert, slot_start, gain,
                   gpsimd_too):
    HB, HT, T0, HS, S0 = portion(h)
    std = sb("std_r", [P, HT], F32)
    rstd = sb("rstd_r", [P, HT], F32)
    w_r = sb("w_r", [P, E], F32)
    b_r = sb("b_r", [P, E], F32)
    zt = sb("r_zt", [P, 2, HALF], F32)
    before = sb("before", [P, P], BF16)
    ones = sb("ones", [P, P], BF16)
    rank = sb("rank", [P, E], F32)
    slot_no = sb("slot_no", [P, HS], F32)
    logit = sb("logit", [P, HT, E], F32)
    prob = sb("prob", [P, HT, E], F32)
    work = sb("work", [P, HT, E], F32)
    chosen = sb("chosen", [P, HT, E], BF16)
    col = [sb(f"col{i}", [P, HT], F32) for i in range(6)]
    keep = sb("keep", [P, E, HT], F32)
    count = sb("count", [P, E, HT], F32)
    upto = sb("upto", [P, E, HT], F32)
    total = sb("total", [P, E], F32)
    total_i = sb("total_i", [P, E], I32)
    tiles_i = sb("tiles_i", [P, E], I32)
    tiles_e = sb("tiles_e", [P, E], F32)
    end_e = sb("end_e", [P, E], F32)
    base_e = sb("base_e", [P, E], F32)
    ones_e = sb("ones_e", [P, E], F32)
    past = sb("past", [P, HS, E], F32)
    slot_f = sb("slot_f", [P, HS], F32)
    ps_t = [psum(f"r_turn{i}", [P, HALF], F32) for i in range(2)]
    ps_logit = psum("ps_logit", [P, HT * E], F32)
    ps_before = psum("ps_before", [P, HT * E], F32)
    ps_count = psum("ps_count", [P, HT * E], F32)
    s_w = sem("r_w")
    s_c = sem("r_c")
    s_var = sem("r_var")
    s_std = sem("r_std")
    s_rstd = sem("r_rstd")
    s_z = sem("r_z")
    s_turn = sem("r_turn")
    s_zt = sem("r_zt")
    s_logit = sem("r_logit")
    s_shift = sem("r_shift")
    s_exp = sem("r_exp")
    s_chosen = sem("r_chosen")
    s_sum = sem("r_sum")
    s_v = sem("r_v")

    with nc.Block() as block:
        @block.sync
        def _(sp):
            sp.dma_start(w_r[:, :], wr).then_inc(s_w, 16)
            sp.dma_start(b_r[:, :], br.partition_broadcast(P)).then_inc(s_w, 16)

        @block.gpsimd
        def _(pool):
            pool.memset(before[:, :], 1.0).then_inc(s_c, 1)
            pool.memset(ones[:, :], 1.0).then_inc(s_c, 1)
            pool.memset(ones_e[:, :], 1.0).then_inc(s_c, 1)
            pool.memset(keep[:, :, 1:HT], 1.0).then_inc(s_c, 1)
            pool.memset(keep[:, :, 0:1], 0.0).then_inc(s_c, 1)
            pool.iota(rank[:, :], [[-1, E]], base=E, channel_multiplier=0,
                      allow_small_or_imprecise_dtypes=True).then_inc(s_c, 1)
            pool.iota(slot_no[:, :], [[1, HS]], base=0, channel_multiplier=0,
                      allow_small_or_imprecise_dtypes=True).then_inc(s_c, 1)
            pool.wait_ge(s_c, 7)
            pool.affine_select(out=before[:, :], in_=before[:, :], compare_op=ALU.is_gt, fill=0.0, base=0,
                               pattern=[[1, P]], channel_multiplier=-1).then_inc(s_c, 1)
            gpsimd_too(pool)

        @block.tensor
        def _(pe):
            pe.wait_ge(s_w, 32)
            for n in range(2 * HB + 1):
                if n < 2 * HB:
                    pe.wait_ge(s_z, n * 4 + 4)
                    if n >= 2:
                        pe.wait_ge(s_zt, n - 1)
                    for q in range(4):
                        mm = pe.transpose(ps_t[n % 2][:, q * P:(q + 1) * P], z_all[:, T0 + 4 * n + q, :], ident[:, :])
                    mm.then_inc(s_turn, 1)
                if n:
                    pe.wait_ge(s_zt, n)
                    for q in range(4):
                        t = 4 * (n - 1) + q
                        mm = pe.matmul(ps_logit[:, t * E:(t + 1) * E], zt[:, (n - 1) % 2, q * P:(q + 1) * P], w_r[:, :],
                                       start=True, stop=True)
                    mm.then_inc(s_logit, 1)
            pe.wait_ge(s_chosen, 1)
            pe.wait_ge(s_c, 8)
            flat = chosen[:, :, :].rearrange("p t e -> p (t e)")
            pe.matmul(ps_before[:, :], before[:, :], flat, start=True, stop=True).then_inc(s_sum, 1)
            pe.matmul(ps_count[:, :], ones[:, :], flat, start=True, stop=True).then_inc(s_sum, 1)

        @block.scalar
        def _(act):
            roots(act, std, s_var, s_std)
            for n in range(2 * HB):
                act.wait_ge(s_turn, n + 1)
                if n >= 2:
                    act.wait_ge(s_logit, n - 1)
                act.activation(zt[:, n % 2, :], ps_t[n % 2][:, :], ACT.Copy).then_inc(s_zt, 1)
            act.wait_ge(s_shift, 1)
            act.activation(prob[:, :, :], logit[:, :, :], ACT.Exp).then_inc(s_exp, 1)

        @block.vector
        def _(dve):
            steps = [0]

            def step(instruction):
                steps[0] += 1
                instruction.then_inc(s_v, 1)
                dve.wait_ge(s_v, steps[0])

            def over_e(column):
                return column.unsqueeze(2).broadcast_to([P, HT, E])

            variances(dve, mv, std, h, s_var)
            inverses(dve, std, rstd, s_std, s_rstd)
            dve.wait_ge(s_rstd, 1)
            with dve.Fori(0, HB) as b:
                for k in range(KT):
                    normalise(dve, tile_of(z_all, b * KT + (T0 + k)), t_all, mv, rstd, h, b * KT + k).then_inc(s_z, 1)
            dve.wait_ge(s_w, 32)
            dve.wait_ge(s_c, 8)
            dve.wait_ge(s_logit, 2 * HB)
            step(dve.tensor_tensor(work[:, :, :], ps_logit[:, :].rearrange("p (t e) -> p t e", e=E),
                                   b_r[:, :].unsqueeze(1).broadcast_to([P, HT, E]), ALU.add))
            step(dve.tensor_reduce(col[0][:, :], work[:, :, :], AX.X, ALU.max))
            dve.tensor_tensor(logit[:, :, :], work[:, :, :], over_e(col[0][:, :]), ALU.subtract).then_inc(s_shift, 1)
            dve.wait_ge(s_exp, 1)
            step(dve.tensor_reduce(col[1][:, :], prob[:, :, :], AX.X, ALU.add))
            step(dve.reciprocal(col[2][:, :], col[1][:, :]))
            step(dve.tensor_tensor(work[:, :, :], prob[:, :, :], over_e(col[2][:, :]), ALU.mult))
            step(dve.tensor_reduce(col[3][:, :], work[:, :, :], AX.X, ALU.max))
            step(dve.reciprocal(col[4][:, :], col[3][:, :]))
            step(dve.tensor_tensor(gain[:, T0:T0 + HT], col[3][:, :], col[4][:, :], ALU.mult))
            step(dve.tensor_tensor(prob[:, :, :], work[:, :, :], over_e(col[3][:, :]), ALU.is_ge))
            step(dve.tensor_tensor(work[:, :, :], prob[:, :, :], rank[:, :].unsqueeze(1).broadcast_to([P, HT, E]),
                                   ALU.mult))
            step(dve.tensor_reduce(col[5][:, :], work[:, :, :], AX.X, ALU.max))
            dve.tensor_tensor(chosen[:, :, :], work[:, :, :], over_e(col[5][:, :]), ALU.is_ge).then_inc(s_chosen, 1)
            dve.wait_ge(s_sum, 2)
            step(dve.tensor_copy(count[:, :, :], ps_count[:, :].rearrange("p (t e) -> p e t", e=E)))
            step(dve.tensor_tensor_scan(upto[:, :, :].rearrange("p e t -> p (e t)"),
                                        keep[:, :, :].rearrange("p e t -> p (e t)"),
                                        count[:, :, :].rearrange("p e t -> p (e t)"), 0.0, ALU.mult, ALU.add))
            step(dve.tensor_scalar(total_i[:, :], upto[:, :, HT - 1], float(P - 1), None, ALU.add))
            step(dve.tensor_scalar(tiles_i[:, :], total_i[:, :], 7, None, ALU.arith_shift_right))
            step(dve.tensor_copy(tiles_e[:, :], tiles_i[:, :]))
            step(dve.tensor_tensor_scan(end_e[:, :], ones_e[:, :], tiles_e[:, :], 0.0, ALU.mult, ALU.add))
            step(dve.tensor_tensor(total[:, :], end_e[:, :], tiles_e[:, :], ALU.subtract))
            step(dve.tensor_scalar(base_e[:, :], total[:, :], float(P), float(S0 * P), ALU.mult, ALU.add))
            step(dve.tensor_tensor(upto[:, :, :], upto[:, :, :], count[:, :, :], ALU.subtract))
            step(dve.tensor_tensor(count[:, :, :], upto[:, :, :], base_e[:, :].unsqueeze(2).broadcast_to([P, E, HT]),
                                   ALU.add))
            step(dve.tensor_tensor(upto[:, :, :], count[:, :, :], ps_before[:, :].rearrange("p (t e) -> p e t", e=E),
                                   ALU.add))
            step(dve.tensor_tensor(work[:, :, :], upto[:, :, :].rearrange("p e t -> p t e"), chosen[:, :, :], ALU.mult))
            step(dve.tensor_reduce(col[0][:, :], work[:, :, :], AX.X, ALU.add))
            dve.tensor_copy(pos[:, T0:T0 + HT], col[0][:, :])
            step(dve.tensor_scalar(pos_out[:, T0:T0 + HT], col[0][:, :], float(-S0 * P), None, ALU.add))
            step(dve.tensor_tensor(past[:, :, :], slot_no[:, :].unsqueeze(2).broadcast_to([P, HS, E]),
                                   end_e[:, :].unsqueeze(1).broadcast_to([P, HS, E]), ALU.is_ge))
            step(dve.tensor_reduce(slot_f[:, :], past[:, :, :], AX.X, ALU.add))
            dve.tensor_scalar(slot_expert[:, S0:S0 + HS], slot_f[:, :], float(E - 1), None, ALU.min)
            step(dve.tensor_scalar(slot_start[:, S0:S0 + HS], slot_f[:, :], float(E - 1), float(HID), ALU.min, ALU.mult))


def expert_kernel(nc, sb, psum, sem, weights, s_ew, s_sent, s_early, ident, slot_expert, slot_start, rows_in, rows_out,
                  gpsimd_too):
    w1_sb, b1_sb, w2_sb, b2_sb = weights
    w1_flat = w1_sb[:, :, :].rearrange("p e n -> p (e n)")
    w2_flat = w2_sb[:, :, :, :].rearrange("p e k c -> p (e k c)")
    RING = 4
    x_in = sb("x_in", [P, RING, C], F32)
    xt = sb("xt", [P, 2, P], F32)
    hid_b = sb("hid_b", [P, 2, HID], F32)
    hid = sb("hid", [P, 2, HID], F32)
    hid_t = sb("hid_t", [P, 2, HID], F32)
    y = sb("y", [P, RING, C], F32)
    ps_x = [psum(f"ps_x{i}", [P, HALF], F32) for i in range(2)]
    ps_h = [psum(f"ps_h{i}", [P, HALF], F32) for i in range(2)]
    ps_t = [psum(f"ps_t{i}", [P, HALF], F32) for i in range(2)]
    ps_y = [psum(f"ps_y{i}", [P, HALF], F32) for i in range(2)]
    s_x = [sem(f"e_x{i}") for i in range(RING)]
    s_turn = sem("e_turn")
    s_xt = sem("e_xt")
    s_up = sem("e_up")
    s_bias = sem("e_bias")
    s_gelu = sem("e_gelu")
    s_ht = sem("e_ht")
    s_htc = sem("e_htc")
    s_down = sem("e_down")
    s_y = sem("e_y")
    s_st = [sem(f"e_st{i}") for i in range(RING)]
    AHEAD = 6
    assert (SLOTS - AHEAD) % RING == 0
    ROUNDS = (SLOTS - AHEAD) // RING
    TURNOVER = (SECOND + 3 - AHEAD) // RING
    assert (SECOND + 3 - AHEAD) % RING == 0
    FETCH = (SECOND - 3 - AHEAD) // RING

    def rounds(i, n):
        return i + n // RING

    with nc.Block() as block:
        @block.sync
        def _(sp):
            def row(s):
                return s * P if isinstance(s, int) else sp.snap(s * P)

            def load(s, r, turned=None):
                first = row(s)
                if turned is not None:
                    sp.wait_ge(s_turn, turned)
                sp.dma_start(x_in[:, r, :], rows_in[bass.ds(first, P), :]).then_inc(s_x[r], 16)

            def store(s, r, h):
                first = row(s - portion(h)[4])
                sp.wait_ge(s_y, s + 1)
                sp.dma_start(rows_out[h][bass.ds(first, P), :], y[:, r, :]).then_inc(s_st[r], 16)

            sp.wait_ge(s_sent[0], 16 * portion(0)[1])
            for s in range(RING):
                load(s, s)

            for s in range(1, AHEAD):
                load(s + 3, (s + 3) % RING, s)
                if s >= 3:
                    store(s - 3, (s - 3) % RING, 0)

            def round_of(i, h):
                for j in range(RING):
                    n = AHEAD + j
                    load(i * RING + (n + 3), (n + 3) % RING, i * RING + n)
                    store(i * RING + (n - 3), (n - 3) % RING, h)

            with sp.Fori(0, FETCH) as i:
                round_of(i, 0)
            sp.wait_ge(s_sent[1], 16 * portion(1)[1])
            with sp.Fori(FETCH, TURNOVER) as i:
                round_of(i, 0)
            for r in range(RING):
                sp.wait_ge(s_st[r], 16 * len(range(r, SECOND, RING)))
            sp.sem_inc(s_early, 1)
            with sp.Fori(TURNOVER, ROUNDS - 1) as i:
                round_of(i, 1)
            for s in range(SLOTS - RING, SLOTS):
                if s + 3 <= SLOTS:
                    load(s + 3, (s + 3) % RING, s)
                store(s - 3, (s - 3) % RING, 1)
            for s in range(SLOTS - 3, SLOTS):
                store(s, s % RING, 1)

            for r in range(RING):
                sp.wait_ge(s_st[r], 16 * len(range(r, SLOTS, RING)))

        @block.gpsimd
        def _(pool):
            gpsimd_too(pool)

        @block.tensor
        def _(pe):
            def turn(s, n, i):
                pe.wait_ge(s_x[n % RING], rounds(i, n) * 16 + 16)
                if n >= 2:
                    pe.wait_ge(s_xt, s - 1)
                pe.transpose(ps_x[n % 2][:, 0:P], x_in[:, n % RING, :], ident[:, :]).then_inc(s_turn, 1)

            def start_of(s):
                return pe.value_load(slot_start[0:1, bass.ds(s, 1)], min_val=0, max_val=(E - 1) * HID)

            def up(s, n, start):
                pe.wait_ge(s_xt, s + 1)
                if n >= 2:
                    pe.wait_ge(s_bias, s - 1)
                pe.matmul(ps_h[n % 2][:, :], xt[:, n % 2, :], w1_flat[:, bass.ds(start, HID)],
                          start=True, stop=True).then_inc(s_up, 1)

            def hidden_turn(s, n):
                pe.wait_ge(s_gelu, s + 1)
                if n >= 2:
                    pe.wait_ge(s_htc, s - 1)
                for k in range(HC):
                    mm = pe.transpose(ps_t[n % 2][:, k * P:(k + 1) * P], hid[:, n % 2, k * P:(k + 1) * P], ident[:, :])
                mm.then_inc(s_ht, 1)

            def down(s, n, start):
                pe.wait_ge(s_htc, s + 1)
                if n >= 2:
                    pe.wait_ge(s_y, s - 1)
                for k in range(HC):
                    mm = pe.matmul(ps_y[n % 2][:, 0:C], hid_t[:, n % 2, k * P:(k + 1) * P],
                                   w2_flat[:, bass.ds(start + k * C, C)], start=(k == 0), stop=(k == HC - 1))
                mm.then_inc(s_down, 1)

            pe.wait_ge(s_ew, 64)
            turn(0, 0, 0)
            up(0, 0, start_of(0))
            turn(1, 1, 0)

            regs = [pe.alloc_register(f"start{k}") for k in range(AHEAD + 2)]

            def bodies(s, n, i, count):
                back = min(n, 2)
                pe.load(regs[0:back + count], slot_start[0:1, bass.ds(s - back, back + count)])
                start = {j - back: pe.snap(regs[j], min_val=0, max_val=(E - 1) * HID) for j in range(back + count)}
                for j in range(count):
                    up(s + j, n + j, start[j])
                    turn(s + (j + 1), n + (j + 1), i)
                    hidden_turn(s + (j - 1), n + (j - 1))
                    if n + j >= 2:
                        down(s + (j - 2), n + (j - 2), start[j - 2])

            bodies(1, 1, 0, AHEAD - 1)
            with pe.Fori(0, ROUNDS) as i:
                bodies(i * RING + AHEAD, AHEAD, i, RING)
            s = SLOTS - 1
            hidden_turn(s, s)
            down(s - 1, s - 1, start_of(s - 1))
            down(s, s, start_of(s))

        @block.scalar
        def _(act):
            def copy_xt(s, n):
                act.wait_ge(s_turn, s + 1)
                if n >= 2:
                    act.wait_ge(s_up, s - 1)
                act.activation(xt[:, n % 2, :], ps_x[n % 2][:, 0:P], ACT.Copy).then_inc(s_xt, 1)

            def gelu(s, n):
                act.wait_ge(s_bias, s + 1)
                if n >= 2:
                    act.wait_ge(s_ht, s - 1)
                act.activation(hid[:, n % 2, :], hid_b[:, n % 2, :], ACT.Gelu).then_inc(s_gelu, 1)

            copy_xt(0, 0)
            copy_xt(1, 1)
            gelu(0, 0)

            def body(s, n):
                copy_xt(s + 1, n + 1)
                gelu(s, n)

            for s in range(1, AHEAD):
                body(s, s)
            with act.Fori(0, ROUNDS) as i:
                for j in range(RING):
                    body(i * RING + (AHEAD + j), AHEAD + j)

        @block.vector
        def _(dve):
            regs = [dve.alloc_register(f"expert{k}") for k in range(AHEAD + 2)]

            def experts(s, n, count):
                back = min(n, 2)
                dve.load(regs[0:back + count], slot_expert[0:1, bass.ds(s - back, back + count)])
                return {j - back: dve.snap(regs[j], min_val=0, max_val=E - 1) for j in range(back + count)}

            def bias(s, n, e):
                dve.wait_ge(s_up, s + 1)
                if n >= 2:
                    dve.wait_ge(s_gelu, s - 1)
                dve.tensor_tensor(hid_b[:, n % 2, :], ps_h[n % 2][:, :], tile_of(b1_sb, e), ALU.add).then_inc(s_bias, 1)

            def copy_ht(s, n):
                dve.wait_ge(s_ht, s + 1)
                if n >= 2:
                    dve.wait_ge(s_down, s - 1)
                dve.tensor_copy(hid_t[:, n % 2, :], ps_t[n % 2][:, :]).then_inc(s_htc, 1)

            def result(s, n, i, e):
                dve.wait_ge(s_down, s + 1)
                if n >= RING:
                    dve.wait_ge(s_st[n % RING], rounds(i, n) * 16)
                dve.tensor_tensor(y[:, n % RING, :], ps_y[n % 2][:, 0:C], tile_of(b2_sb, e), ALU.add).then_inc(s_y, 1)

            dve.wait_ge(s_ew, 64)
            bias(0, 0, experts(0, 0, 1)[0])

            def bodies(s, n, i, count):
                of = experts(s, n, count)
                for j in range(count):
                    bias(s + j, n + j, of[j])
                    copy_ht(s + (j - 1), n + (j - 1))
                    if n + j >= 2:
                        result(s + (j - 2), n + (j - 2), i, of[j - 2])

            bodies(1, 1, 0, AHEAD - 1)
            with dve.Fori(0, ROUNDS) as i:
                bodies(i * RING + AHEAD, AHEAD, i, RING)
            s = SLOTS - 1
            copy_ht(s, s)
            of = experts(s, s, 1)
            result(s - 1, s - 1, 0, of[-1])
            result(s, s, 0, of[0])


def scatter(pool, h, t, z_all, pos, rows_in, s_sent):
    pool.indirect_dma_start(rows_in, bass.IndirectOffsetOnAxis(ap=pos[:, t:t + 1], axis=0),
                            z_all[:, t, :], None).then_inc(s_sent[h], 16)


def gather(pool, h, z_all, pos_out, rows_out, s_sent, s_back):
    _, HT, T0, _, _ = portion(h)
    pool.wait_ge(s_sent[h], 16 * HT)
    for t in range(T0, T0 + HT):
        pool.indirect_dma_start(z_all[:, t, :], None, rows_out[h],
                                bass.IndirectOffsetOnAxis(ap=pos_out[:, t:t + 1], axis=0)).then_inc(s_back[t // KT], 16)


def result_kernel(nc, sb, psum, sem, z_all, t_all, gain, ident, out, s_back, gpsimd_too):
    RING = 4
    out_t = sb("out_t", [P, RING, HALF], F32)
    ps = [psum(f"ps_out{i}", [P, HALF], F32) for i in range(RING)]
    s_add = sem("o_add")
    s_ot = sem("o_turn")
    s_oc = sem("o_copy")
    s_out = [sem(f"o_out{i}") for i in range(RING)]
    with nc.Block() as block:
        @block.gpsimd
        def _(pool):
            gpsimd_too(pool)

        @block.vector
        def _(dve):
            for t in range(TILES):
                dve.wait_ge(s_back[t // KT], 16 * KT)
                dve.scalar_tensor_tensor(out=t_all[:, t, :], in0=z_all[:, t, :], scalar=gain[:, t:t + 1],
                                         in1=t_all[:, t, :], op0=ALU.mult, op1=ALU.add).then_inc(s_add, 1)

        @block.tensor
        def _(pe):
            for n in range(2 * B):
                pe.wait_ge(s_add, 4 * (n + 1))
                if n >= RING:
                    pe.wait_ge(s_oc, n - RING + 1)
                for q in range(4):
                    mm = pe.transpose(ps[n % RING][:, q * P:(q + 1) * P], t_all[:, 4 * n + q, :], ident[:, :])
                mm.then_inc(s_ot, 1)

        @block.scalar
        def _(act):
            for n in range(2 * B):
                act.wait_ge(s_ot, n + 1)
                if n >= RING:
                    act.wait_ge(s_out[n % RING], 16 * (n // RING))
                act.activation(out_t[:, n % RING, :], ps[n % RING][:, :], ACT.Copy).then_inc(s_oc, 1)

        @block.sync
        def _(sp):
            for n in range(2 * B):
                sp.wait_ge(s_oc, n + 1)
                sp.dma_start(out[n // 2, :, n % 2 * HALF:(n % 2 + 1) * HALF],
                             out_t[:, n % RING, :]).then_inc(s_out[n % RING], 16)
            for r in range(RING):
                sp.wait_ge(s_out[r], 16 * len(range(r, 2 * B, RING)))


def build(nc, x, w_proj, b_proj, w_out, b_out, wq, wk, wv, wr, br, w1, b1, w2, b2, out):
    rows_in = nc.dram_tensor("rows_in", [(SLOTS + 1) * P, C], F32).ap()
    rows_out = [nc.dram_tensor(f"rows_out{h}", [portion(h)[3] * P, C], F32).ap() for h in range(2)]
    parts_dram = nc.dram_tensor("parts_dram", [2, G, 3, GROWS, N], BF16).ap()

    def allocators(ctx, tag=""):
        return (lambda n, s, d: ctx.enter_context(nc.sbuf_tensor(n + tag, s, d)),
                lambda n, s, d: ctx.enter_context(nc.psum_tensor(n + tag, s, d)),
                lambda n: ctx.enter_context(nc.semaphore(n + tag)))

    with ExitStack() as top:
        sb, _, sem = allocators(top)
        t_all = sb("t_all", [P, TILES, C], F32)
        ident = sb("ident", [P, P], F32)
        identb = sb("identb", [P, P], BF16)
        stats = sb("stats", [P, KT, 6], F32)
        mv_batch = sb("mv_batch", [P, KT, 2], F32)
        mv_a = sb("mv_a", [P, TILES, 2], F32)
        mv_b = sb("mv_b", [P, TILES, 2], F32)
        with ExitStack() as ctx:
            attention_kernel(nc, *allocators(ctx), x, w_proj, b_proj, w_out, b_out, t_all, stats, mv_batch, mv_a,
                             ident, identb, parts_dram)
        zeros = sb("zeros", [P, C], F32)
        w_t = sb("w_t", [P, 3, C], F32)
        z_all = sb("z_all", [P, TILES, C], F32)
        pos = sb("pos", [P, TILES], U32)
        pos_out = sb("pos_out", [P, TILES], U32)
        gain = sb("gain", [P, TILES], F32)
        slot_expert = sb("slot_expert", [P, SLOTS], I32)
        slot_start = sb("slot_start", [P, SLOTS], I32)
        w1_sb = sb("w1_sb", [P, E, HID], F32)
        w2_sb = sb("w2_sb", [P, E, HC, C], F32)
        b1_sb = sb("b1_sb", [P, E, HID], F32)
        b2_sb = sb("b2_sb", [P, E, C], F32)
        s_ew = sem("e_w")
        s_clear = sem("e_clear")
        s_zero = sem("e_zero")
        s_early = sem("e_early")
        s_sent = [sem(f"e_sent{h}") for h in range(2)]
        s_back = [sem(f"e_back{b}") for b in range(B)]

        def clear_and_load(sp):
            sp.wait_ge(s_clear, 1)
            sp.dma_start(rows_in.rearrange("(s p) c -> p s c", p=P),
                         zeros[:, :].unsqueeze(1).broadcast_to([P, SLOTS + 1, C])).then_inc(s_zero, 16)
            sp.dma_start(w1_sb[:, :, :], w1.rearrange("e c h -> c e h")).then_inc(s_ew, 16)
            sp.dma_start(w2_sb[:, :, :, :], w2.rearrange("e (k p) c -> p e k c", p=P)).then_inc(s_ew, 16)
            sp.dma_start(b1_sb[:, :, :], b1.partition_broadcast(P)).then_inc(s_ew, 16)
            sp.dma_start(b2_sb[:, :, :], b2.partition_broadcast(P)).then_inc(s_ew, 16)

        def clear_zeros(pool):
            pool.memset(zeros[:, :], 0.0).then_inc(s_clear, 1)

        sent_beside = portion(0)[1] * 3 // 5

        def send_first(pool):
            pool.wait_ge(s_zero, 16)
            for t in range(sent_beside):
                scatter(pool, 0, t, z_all, pos, rows_in, s_sent)

        def send_rest(pool):
            for t in range(sent_beside, portion(0)[1]):
                scatter(pool, 0, t, z_all, pos, rows_in, s_sent)

        for h in range(2):
            with ExitStack() as ctx:
                spike_kernel(nc, *allocators(ctx, f"_{h}"), h, w_t, wq, wk, wv, t_all, mv_a, stats, mv_batch, mv_b, ident,
                             clear_and_load if h == 0 else lambda sp: None, send_first if h else clear_zeros)
            with ExitStack() as ctx:
                routing_kernel(nc, *allocators(ctx, f"_{h}"), h, wr, br, t_all, z_all, mv_b, ident, pos, pos_out,
                               slot_expert, slot_start, gain, send_rest if h else lambda pool: None)
        def send_second_fetch_first(pool):
            for t in range(portion(0)[1], TILES):
                scatter(pool, 1, t, z_all, pos, rows_in, s_sent)
            pool.wait_ge(s_early, 1)
            gather(pool, 0, z_all, pos_out, rows_out, s_sent, s_back)

        with ExitStack() as ctx:
            expert_kernel(nc, *allocators(ctx), (w1_sb, b1_sb, w2_sb, b2_sb), s_ew, s_sent, s_early, ident, slot_expert,
                          slot_start, rows_in, rows_out, send_second_fetch_first)
        with ExitStack() as ctx:
            result_kernel(nc, *allocators(ctx), z_all, t_all, gain, ident, out, s_back,
                          lambda pool: gather(pool, 1, z_all, pos_out, rows_out, s_sent, s_back))


_INS = ['x', 'L0_conv_w_proj', 'L0_conv_b_proj', 'L0_conv_w_out', 'L0_conv_b_out', 'L1_attn_Wq', 'L1_attn_Wk',
        'L1_attn_Wv', 'L1_ffn_Wr', 'L1_ffn_br', 'L1_ffn_W1', 'L1_ffn_b1', 'L1_ffn_W2', 'L1_ffn_b2']


def kernel(**inputs):
    import numpy as _np
    import concourse.bacc as _bacc
    from concourse.bass_utils import run_bass_kernel_spmd as _run

    nc = _bacc.Bacc("TRN2", target_bir_lowering=False, num_devices=1)
    arrays, args = {}, []
    for name in _INS:
        a = _np.ascontiguousarray(inputs[name])
        if name == 'x':
            a = a.reshape(B, C, N)
        arrays[f"in_{name}"] = a
        args.append(nc.dram_tensor(f"in_{name}", a.shape, mybir.dt.from_np(a.dtype), kind="ExternalInput").ap())
    args.append(nc.dram_tensor("out_0", (B, C, N), F32, kind="ExternalOutput").ap())
    build(nc, *args)
    r = _run(nc, [arrays], core_ids=[0])
    return r.results[0]["out_0"].reshape(B, C, 32, 32)
```
